# Optimizing a Trainium2 kernel written in Bass

```python
import numpy as np
import jax
import jax.numpy as jnp

def _softmax(x, axis=-1):
    return jax.nn.softmax(x, axis=axis)

def _gelu(x):
    return jax.nn.gelu(x, approximate=True)

def _silu(x):
    return jax.nn.silu(x)

def _sigmoid(x):
    return jax.nn.sigmoid(x)

def _layernorm(x, axis=-1, eps=1e-05):
    m = jnp.mean(x, axis=axis, keepdims=True)
    v = jnp.var(x, axis=axis, keepdims=True)
    return (x - m) / jnp.sqrt(v + eps)

def _scatter_add(tgt, idx, src, axis=0):
    return tgt.at[idx].add(src)

def _segment_sum(src, seg, n):
    return jax.ops.segment_sum(src, seg, n)
kernel_name = 'mk_xattn_ffn_d1_seqx_r8_015368'

def setup_inputs(seed: int=0):
    np.random.seed(seed)
    _w = jnp.asarray

    def _rec_inputs():
        import jax
        import jax.numpy as jnp
        _rk = jax.random.key(seed)
        x = 7.22e-05 + 1 * jax.random.normal(jax.random.fold_in(_rk, 1), (16, 256, 128), jnp.float32)
        _lenS = 256 - jax.random.randint(jax.random.fold_in(_rk, 7), (16,), 0, max(1, 256 // 4) + 1, jnp.int32)
        _lenS2 = 64 - jax.random.randint(jax.random.fold_in(_rk, 8), (16,), 0, max(1, 64 // 4) + 1, jnp.int32)
        _ctx_768P = jax.random.normal(jax.random.fold_in(_rk, 11), (16, 16, 96), jnp.float32)
        _ctx_768c = jax.random.dirichlet(jax.random.fold_in(_rk, 511), 0.3 * jnp.ones((16,), jnp.float32), (16, 64))
        _ctx_768t = jnp.einsum('bsk,bkd->bsd', _ctx_768c, _ctx_768P)
        _ctx_768t = _ctx_768t * jax.lax.rsqrt(jnp.mean(jnp.square(_ctx_768t)) + 1e-12) * 0.953939
        ctx_768 = 2.09791e-05 + 1.00001 * (_ctx_768t + 0.3 * jax.random.normal(jax.random.fold_in(_rk, 611), (16, 64, 96), jnp.float32))
        return (x, ctx_768)
    x, ctx_768 = _rec_inputs()

    def _L0_xattn_setup():
        import jax, jax.numpy as jnp
        import numpy as np
        HEADS = 8
        DIM_HEAD = 64
        SCALE = DIM_HEAD ** (-0.5)
        key = jax.random.key(seed)
        ks = jax.random.split(key, 7)
        b, n, m = (4, 256, 128)
        qd, cd, inner = (128, 96, HEADS * DIM_HEAD)
        s = lambda fan_in: 1.0 / np.sqrt(fan_in)
        return {'x': jax.random.normal(ks[0], (b, n, qd), jnp.float32), 'context': jax.random.normal(ks[1], (b, m, cd), jnp.float32), 'Wq': jax.random.normal(ks[2], (qd, inner), jnp.float32) * s(qd), 'Wk': jax.random.normal(ks[3], (cd, inner), jnp.float32) * s(cd), 'Wv': jax.random.normal(ks[4], (cd, inner), jnp.float32) * s(cd), 'Wout': jax.random.normal(ks[5], (inner, qd), jnp.float32) * s(inner), 'bout': jax.random.normal(ks[6], (qd,), jnp.float32) * 0.01}
    _L0_xattn_all = _L0_xattn_setup()
    _L0_xattn_in = {k: v for k, v in _L0_xattn_all.items() if k in ('Wq', 'Wk', 'Wv', 'Wout', 'bout')}
    del _L0_xattn_all

    def _L0_ffn_setup():
        import jax, jax.numpy as jnp
        import numpy as np
        B, S, D = (2, 256, 128)
        M = 256
        E = 8
        TOP_K = 2
        key = jax.random.key(seed)
        ks = jax.random.split(key, 5)
        std = 0.02
        return {'residual': jax.random.normal(ks[0], (B, S, D), jnp.float32), 'W_router': jax.random.normal(ks[1], (D, E), jnp.float32) * std, 'W_gate': jax.random.normal(ks[2], (E, D, M), jnp.float32) * std, 'b_gate': jnp.zeros((E, M), jnp.float32), 'W_up': jax.random.normal(ks[3], (E, D, M), jnp.float32) * std, 'b_up': jnp.zeros((E, M), jnp.float32), 'W_out': jax.random.normal(ks[4], (E, M, D), jnp.float32) * std, 'b_out': jnp.zeros((E, D), jnp.float32)}
    _L0_ffn_all = _L0_ffn_setup()
    _L0_ffn_in = {k: v for k, v in _L0_ffn_all.items() if k in ('W_router', 'W_gate', 'b_gate', 'W_up', 'b_up', 'W_out', 'b_out')}
    del _L0_ffn_all
    return {'x': x, 'ctx_768': ctx_768, 'L0_xattn_Wq': _L0_xattn_in['Wq'], 'L0_xattn_Wk': _L0_xattn_in['Wk'], 'L0_xattn_Wv': _L0_xattn_in['Wv'], 'L0_xattn_Wout': _L0_xattn_in['Wout'], 'L0_xattn_bout': _L0_xattn_in['bout'], 'L0_ffn_W_router': _L0_ffn_in['W_router'], 'L0_ffn_W_gate': _L0_ffn_in['W_gate'], 'L0_ffn_b_gate': _L0_ffn_in['b_gate'], 'L0_ffn_W_up': _L0_ffn_in['W_up'], 'L0_ffn_b_up': _L0_ffn_in['b_up'], 'L0_ffn_W_out': _L0_ffn_in['W_out'], 'L0_ffn_b_out': _L0_ffn_in['b_out']}

def reference(x, ctx_768, L0_xattn_Wq, L0_xattn_Wk, L0_xattn_Wv, L0_xattn_Wout, L0_xattn_bout, L0_ffn_W_router, L0_ffn_W_gate, L0_ffn_b_gate, L0_ffn_W_up, L0_ffn_b_up, L0_ffn_W_out, L0_ffn_b_out):
    import jax
    import jax.numpy as jnp

    def _L0_xattn_ref(x, context, Wq, Wk, Wv, Wout, bout):
        import jax, jax.numpy as jnp
        import numpy as np
        HEADS = 8
        DIM_HEAD = 64
        SCALE = DIM_HEAD ** (-0.5)
        b, n, _ = x.shape
        m = context.shape[1]
        q = (x @ Wq).reshape(b, n, HEADS, DIM_HEAD)
        k = (context @ Wk).reshape(b, m, HEADS, DIM_HEAD)
        v = (context @ Wv).reshape(b, m, HEADS, DIM_HEAD)
        sim = jnp.einsum('bihd,bjhd->bhij', q, k) * SCALE
        attn = jax.nn.softmax(sim, axis=-1)
        out = jnp.einsum('bhij,bjhd->bihd', attn, v).reshape(b, n, HEADS * DIM_HEAD)
        return out @ Wout + bout

    def _L0_ffn_ref(residual, W_router, W_gate, b_gate, W_up, b_up, W_out, b_out):
        import jax, jax.numpy as jnp
        import numpy as np
        B, S, D = (2, 256, 128)
        M = 256
        E = 8
        TOP_K = 2
        router_logits = jnp.einsum('bsd,de->bse', residual, W_router)
        router_probs = jax.nn.softmax(router_logits, axis=-1)
        top_k_probs, top_k_idx = jax.lax.top_k(router_probs, TOP_K)
        top_k_probs = top_k_probs / (jnp.sum(top_k_probs, -1, keepdims=True) + 1e-08)
        one_hot = jax.nn.one_hot(top_k_idx, E, dtype=residual.dtype)
        expert_weights = jnp.einsum('bsk,bske->bse', top_k_probs, one_hot)
        gate = jax.nn.silu(jnp.einsum('bsd,edm->ebsm', residual, W_gate) + b_gate[:, None, None, :])
        up = jnp.einsum('bsd,edm->ebsm', residual, W_up) + b_up[:, None, None, :]
        hidden = gate * up
        expert_out = jnp.einsum('ebsm,emd->ebsd', hidden, W_out) + b_out[:, None, None, :]
        output = jnp.einsum('bse,ebsd->bsd', expert_weights, expert_out)
        return output
    x = x + _L0_xattn_ref(_layernorm(x, axis=-1), ctx_768, L0_xattn_Wq, L0_xattn_Wk, L0_xattn_Wv, L0_xattn_Wout, L0_xattn_bout)
    x = x + _L0_ffn_ref(_layernorm(x, axis=-1), L0_ffn_W_router, L0_ffn_W_gate, L0_ffn_b_gate, L0_ffn_W_up, L0_ffn_b_up, L0_ffn_W_out, L0_ffn_b_out)
    return x

_drawn_inputs = setup_inputs


def setup_inputs(seed=0):
    import zlib

    import numpy as np

    out = dict(_drawn_inputs(seed))
    spreads = {'L0_ffn_b_gate': (0.0, 0.8), 'L0_ffn_b_up': (0.0, 0.8), 'L0_ffn_b_out': (0.0, 0.56)}
    factors = {'L0_xattn_bout': 4.985, 'L0_ffn_W_gate': 8.0, 'L0_ffn_W_up': 8.0, 'L0_ffn_W_out': 8.0}
    for name, (base, spread) in spreads.items():
        noise = np.random.default_rng([zlib.crc32(name.encode()), seed]).standard_normal(out[name].shape)
        drawn = base * np.exp(spread * noise) if base else spread * noise
        out[name] = jnp.asarray(drawn.astype(out[name].dtype))
    for name, factor in factors.items():
        out[name] = (out[name] * factor).astype(out[name].dtype)
    return out
```

```python
from contextlib import ExitStack

import concourse.bass as bass
from concourse import mybir

F32 = mybir.dt.float32
F32R = mybir.dt.float32r
U32 = mybir.dt.uint32
ALU = mybir.AluOpType
ACT = mybir.ActivationFunctionType
AX_X = mybir.AxisListType.X

P = 128
EPS = 1e-5
NORM_EPS = 1e-8


def xattn_moe_kernel(nc, x, ctx_in, Wq, Wk, Wv, Wout, bout, Wr, Wg, bg, Wu, bu, Wo, bo, out):
    NB, SEQ, D = x.shape
    _, J, CD = ctx_in.shape
    INNER = Wq.shape[1]
    DH = 64
    H = INNER // DH
    HP = H // 2
    E, _, M = Wg.shape
    MC = M // P
    TOK = 512
    KT = TOK // P
    BT = TOK // SEQ
    NT = NB * SEQ // TOK
    CH = E * MC
    HB = H // 2
    SCALE = DH ** -0.5
    LAG = 3
    WB_PARTS = ((0, 2), (2, 6), (6, 8))
    NHB = 4
    PAIR = 2 * BT * J
    assert D == P and CH == 16 and J * 2 == P and TOK == 512 and NT % 2 == 0 and E == 8 and BT == 2

    x_t = x.rearrange("(t b) (s p) d -> t p (b s) d", b=BT, p=P)
    out_t = out.rearrange("(t b) (s p) d -> t p (b s) d", b=BT, p=P)
    ctxT_dram = [nc.dram_tensor(f"ctxT_{n}_scratch", (CD, (NT + 1) * BT * J), F32, kind="Internal").ap() for n in ("hi", "lo")]
    w_dram = nc.dram_tensor("expert_weights_scratch", (E, TOK), F32, kind="Internal").ap()

    with ExitStack() as stack:
        def sb(name, shape, dt=F32):
            return stack.enter_context(nc.sbuf_tensor(name, shape, dt))

        def sem(name):
            return stack.enter_context(nc.semaphore(name))

        ident = sb("ident", [P, P])
        wg_hi = sb("wg_hi", [P, CH, P], F32R)
        wg_lo = sb("wg_lo", [P, CH, P], F32R)
        wu_hi = sb("wu_hi", [P, CH, P], F32R)
        wu_lo = sb("wu_lo", [P, CH, P], F32R)
        wo_hi = sb("wo_hi", [P, CH, D], F32R)
        wo_lo = sb("wo_lo", [P, CH, D], F32R)
        m_hi = sb("m_hi", [CD, H, D], F32R)
        m_lo = sb("m_lo", [CD, H, D], F32R)
        n_hi = sb("n_hi", [CD, H, D], F32R)
        n_lo = sb("n_lo", [CD, H, D], F32R)
        wr_raw = sb("wr_raw", [P, E])
        wr_hl = sb("wr_hl", [P, 2, E], F32R)
        bout_col = sb("bout_col", [D, 1])
        bgu_raw = sb("bgu_raw", [2 * CH, P])
        bgu = sb("bgu", [P, 2, CH])
        bo_raw = sb("bo_raw", [3 * E, D])
        bo_hi = sb("bo_hi", [3 * E, D], F32R)
        bo_lo = sb("bo_lo", [3 * E, D], F32R)
        bo_hhl = sb("bo_hhl", [3 * E, D], F32R)
        iota_e = sb("iota_e", [P, KT, E])

        x_raw = sb("x_raw", [P, 2, KT, D])
        bn = sb("bn", [P, 2 * KT, 6])
        m_diff = sb("m_diff", [P, 2 * KT])
        m_sq = sb("m_sq", [P, 2 * KT])
        v_sum = sb("v_sum", [P, 2 * KT])
        v_eps = sb("v_eps", [P, 2 * KT])
        var_eps = sb("var_eps", [P, 2 * KT])
        neg_mean = sb("neg_mean", [P, 2 * KT])
        rstd = sb("rstd", [P, 2 * KT])
        nmr = sb("nmr", [P, 2 * KT])
        m_half = sb("m_half", [P, 2 * KT])
        xn = sb("xn", [P, KT, D])
        xnT_hi = sb("xnT_hi", [P, TOK], F32R)
        xnT_lo = sb("xnT_lo", [P, TOK], F32R)
        ctxc_hi = sb("ctxc_hi", [CD, PAIR], F32R)
        ctxc_lo = sb("ctxc_lo", [CD, PAIR], F32R)
        a_hi = sb("a_hi", [P, 2 * BT, H, J], F32R)
        a_lo = sb("a_lo", [P, 2 * BT, H, J], F32R)
        ctxT_hi = a_hi[0:CD, :, :, :].rearrange("p b h j -> p (b h j)")[:, 0:NB * J]
        ctxT_lo = a_lo[0:CD, :, :, :].rearrange("p b h j -> p (b h j)")[:, 0:NB * J]
        bs_hi = sb("bs_hi", [P, H, D], F32R)
        bs_lo = sb("bs_lo", [P, H, D], F32R)
        b_hi = sb("b_hi", [P, BT, HP, D], F32R)
        b_lo = sb("b_lo", [P, BT, HP, D], F32R)
        s_max = sb("s_max", [P, KT, H])
        probs = sb("probs", [P, KT, H, J])
        r_sum = sb("r_sum", [P, KT, H])
        r_inv = sb("r_inv", [P, KT, H])
        pT_hi = sb("pT_hi", [P, HP, TOK], F32R)
        pT_lo = sb("pT_lo", [P, HP, TOK], F32R)
        ot_sb = sb("ot_sb", [P, TOK])
        x1 = sb("x1", [P, 2, KT, D])
        xn2 = sb("xn2", [P, KT, D])
        xn2T_hi = sb("xn2T_hi", [P, 2, TOK], F32R)
        xn2T_lo = sb("xn2T_lo", [P, 2, TOK], F32R)

        lg_lo = sb("lg_lo", [P, KT, E])
        lg = sb("lg", [P, KT, E])
        top = sb("top", [P, KT, 8])
        top_at = sb("top_at", [P, KT, 8], U32)
        lg_d = sb("lg_d", [P, KT, E])
        lg_e = sb("lg_e", [P, KT, E])
        oh1 = sb("oh1", [P, KT, E])
        oh2 = sb("oh2", [P, KT, E])
        sel = sb("sel", [P, KT, E])
        sel_e = sb("sel_e", [P, KT, E])
        den_a = sb("den_a", [P, KT])
        den_b = sb("den_b", [P, KT])
        den = sb("den", [P, KT])
        den_inv = sb("den_inv", [P, KT])
        wst = sb("wst", [P, KT, 4 * E])
        wT = sb("wT", [4 * E, TOK])
        wT_r = sb("wT_r", [4 * E, TOK], F32R)
        wb = sb("wb", [P, E, TOK])

        ffn_tmp = sb("ffn_tmp", [P, 6, TOK])
        h_hi = sb("h_hi", [P, NHB, TOK], F32R)
        h_lo = sb("h_lo", [P, NHB, TOK], F32R)
        yT_sb = sb("yT_sb", [P, TOK])
        y_out = sb("y_out", [P, KT, D])

        def gate_sb(c):
            return ffn_tmp[:, c % 2, :]

        def gw_sb(c):
            return ffn_tmp[:, 2 + c % 2, :]

        def h_sb(c):
            return ffn_tmp[:, 4 + c % 2, :]

        def bank(name):
            return stack.enter_context(nc.psum_tensor(name, [P, 512], F32))

        gate_ps = [bank("gate_ps0"), bank("gate_ps1")]
        up_ps = [bank("up_ps0"), bank("up_ps1")]
        y_ps = bank("y_ps")
        T_ps = bank("T_ps")
        S_ps = bank("S_ps")
        O_ps = bank("O_ps")

        names = (
            "x_loaded attn_w_loaded ctx_loaded small_loaded ffn_w_loaded bo_loaded ident_ready prep_T prep_T_read "
            "prep_ctx_T prep_ctx_hi prep_ctx_lo prep_fold prep_fold_hi prep_fold_lo ctxT_saved ctxc_loaded bgu_T bgu_ready "
            "w_hi_ready w_lo_ready wr_hi_ready wr_ready bo_hi_ready bo_lo_ready bo_ready iota_ready half_ready "
            "ln1_stats ln1_pow ln1_rstd xn_ready xT_ready xT_hi xT_lo "
            "a_ready a_hi_done a_lo_done b_ready b_hi_done b_lo_done b_moved "
            "s_ready s_maxed s_sub exp_done sums_done inv_done norm_done pT_ready pT_hi_done pT_lo_done "
            "ot_ready ot_read ott_ready x1_ready ln2_stats ln2_pow ln2_rstd xn2_ready "
            "x2T_ready x2T_hi x2T_lo router_ready route_step w_steps logits_ready route_exp w_ready wT_ready wT_done "
            "w_saved wb_loaded0 wb_loaded1 wb_loaded2 "
            "gate_ready gate_done gw_done up_ready h_done h_hi_done h_lo_done down_done "
            "y_read yT_ready y_added y_stored"
        ).split()
        S = {n: sem(n) for n in names}

        def wait(eng, name, value):
            if not isinstance(value, int) or value > 0:
                eng.wait_ge(S[name], value)

        def live(t):
            return not isinstance(t, int) or 0 <= t < NT

        def ahead(t):
            return t if isinstance(t, int) else t % NT

        def walk(eng, step):
            for c in range(5, CH):
                step(-2, c, 0)
            for c in range(CH):
                step(-1, c, 1)
            for c in range(5):
                step(0, c, 0)
            with eng.Fori(0, NT // 2 - 1) as pair:
                T = pair * 2
                for c in range(5, CH):
                    step(T, c, 0)
                for c in range(CH):
                    step(T + 1, c, 1)
                for c in range(5):
                    step(T + 2, c, 0)
            for c in range(5, CH):
                step(NT - 2, c, 0)
            for c in range(CH):
                step(NT - 1, c, 1)
            for c in range(5):
                step(NT, c, 0)

        def as_f32(ap):
            return ap.bitcast(F32)

        def folded(n):
            return (S_ps, O_ps, gate_ps[0], gate_ps[1])[n][0:CD, :].rearrange("p (q d) -> p q d", d=D)

        block = stack.enter_context(nc.Block())

        @block.sync
        def _(sp):
            sp.dma_start(x_raw[:, 0, :, :], x_t[0]).then_inc(S["x_loaded"], 16)
            sp.dma_start(probs[:, 0, :, :].rearrange("p h j -> p (h j)"), Wq).then_inc(S["attn_w_loaded"], 16)
            sp.dma_start(probs[0:CD, 1, :, :].rearrange("p h j -> p (h j)"), Wk).then_inc(S["attn_w_loaded"], 16)
            sp.dma_start(x1[:, :, :, :].rearrange("p a k d -> p (a k d)")[:, 0:8 * CD].rearrange("p (s c) -> p s c", c=CD),
                         ctx_in.rearrange("b j c -> (b j) c").rearrange("(s p) c -> p s c", p=P)
                         ).then_inc(S["ctx_loaded"], 16)
            sp.dma_start(probs[0:CD, 2, :, :].rearrange("p h j -> p (h j)"), Wv).then_inc(S["attn_w_loaded"], 16)
            sp.dma_start(probs[:, 3, :, :].rearrange("p h j -> p (h j)").rearrange("p (s d) -> p s d", d=D),
                         Wout.rearrange("(s p) d -> p s d", p=P)).then_inc(S["attn_w_loaded"], 16)
            sp.dma_start(bgu_raw[0:CH, :], bg.rearrange("e (m p) -> (e m) p", p=P)).then_inc(S["small_loaded"], 16)
            sp.dma_start(bgu_raw[CH:2 * CH, :], bu.rearrange("e (m p) -> (e m) p", p=P)).then_inc(S["small_loaded"], 16)
            sp.dma_start(bout_col[:, :], bout.rearrange("(d a) -> d a", a=1)).then_inc(S["small_loaded"], 16)
            sp.dma_start(wr_raw[:, :], Wr).then_inc(S["small_loaded"], 16)
            for n in range(3):
                sp.dma_start(bo_raw[n * E:(n + 1) * E, :], bo).then_inc(S["bo_loaded"], 16)
            sp.dma_start(wb[:, 0:4, :].rearrange("p a n -> p (a n)").rearrange("p (e m) -> p e m", e=E),
                         Wg.rearrange("e p m -> p e m")).then_inc(S["ffn_w_loaded"], 16)
            sp.dma_start(wb[:, 4:8, :].rearrange("p a n -> p (a n)").rearrange("p (e m) -> p e m", e=E),
                         Wu.rearrange("e p m -> p e m")).then_inc(S["ffn_w_loaded"], 16)
            sp.dma_start(ffn_tmp[:, 0:4, :].rearrange("p a n -> p (a n)").rearrange("p (c d) -> p c d", d=D),
                         Wo.rearrange("e (m p) d -> p (e m) d", p=P)).then_inc(S["ffn_w_loaded"], 16)
            sp.wait_ge(S["bo_lo_ready"], 1)
            sp.dma_start(as_f32(bo_hhl[0:2 * E, :]), as_f32(bo_hi[0:2 * E, :])).then_inc(S["bo_ready"], 16)
            sp.dma_start(as_f32(bo_hhl[2 * E:3 * E, :]), as_f32(bo_lo[2 * E:3 * E, :])).then_inc(S["bo_ready"], 16)
            sp.wait_ge(S["prep_ctx_lo"], 2)
            sp.dma_start(ctxT_dram[0][:, 0:NB * J], as_f32(ctxT_hi)).then_inc(S["ctxT_saved"], 16)
            sp.dma_start(ctxT_dram[1][:, 0:NB * J], as_f32(ctxT_lo)).then_inc(S["ctxT_saved"], 16)
            sp.wait_ge(S["ctxT_saved"], 32)
            sp.dma_start(as_f32(ctxc_hi[:, :]), ctxT_dram[0][:, 0:PAIR]).then_inc(S["ctxc_loaded"], 16)
            sp.dma_start(as_f32(ctxc_lo[:, :]), ctxT_dram[1][:, 0:PAIR]).then_inc(S["ctxc_loaded"], 16)
            sp.dma_start(x_raw[:, 1, :, :], x_t[1]).then_inc(S["x_loaded"], 16)

            def step(T, c, odd):
                y_of, main, early = T - 1, T + 1, T + 2

                def index(t):
                    return t if isinstance(t, int) else sp.snap(t)

                if c == 4 and live(y_of):
                    at = index(y_of)
                    sp.wait_ge(S["y_added"], y_of + 1)
                    sp.dma_start(out_t[at], y_out[:, :, :]).then_inc(S["y_stored"], 16)
                if c == 7 and live(main) and live(T + 3):
                    at = index(ahead(T + 3))
                    sp.wait_ge(S["x1_ready"], main * 2 + 2)
                    sp.dma_start(x_raw[:, 1 - odd, :, :], x_t[at]).then_inc(S["x_loaded"], 16)
                if c in (8, 10) and live(early):
                    q = (c - 8) // 2
                    sp.wait_ge(S["b_lo_done"], early * 2 + q + 1)
                    wait(sp, "ot_ready", early * 2)
                    for b in range(BT):
                        for par in range(2):
                            for src, dst in ((bs_hi, b_hi), (bs_lo, b_lo)):
                                sp.dma_start(
                                    as_f32(dst[par * J:(par + 1) * J, b, 2 * q:2 * q + 2, :]),
                                    as_f32(src[b * J:(b + 1) * J, 4 * q:4 * q + 4, :]).rearrange(
                                        "p (n r) d -> p n r d", r=2)[:, :, par, :]).then_inc(S["b_moved"], 16)
                if c == 11 and live(early) and live(T + 3) and odd:
                    at = index(ahead(T + 3) * (BT * J))
                    sp.wait_ge(S["b_ready"], early * 2 + 2)
                    cols = slice(at, at + PAIR) if isinstance(T, int) else bass.ds(at, PAIR)
                    sp.dma_start(as_f32(ctxc_hi[:, :]), ctxT_dram[0][:, cols]).then_inc(S["ctxc_loaded"], 16)
                    sp.dma_start(as_f32(ctxc_lo[:, :]), ctxT_dram[1][:, cols]).then_inc(S["ctxc_loaded"], 16)
                if c == 14 and live(main):
                    sp.wait_ge(S["wT_done"], main + 1)
                    sp.dma_start(w_dram, wT[3 * E:4 * E, :]).then_inc(S["w_saved"], 16)
                    sp.wait_ge(S["w_saved"], main * 16 + 16)
                    if isinstance(main, int) and main == 0:
                        sp.wait_ge(S["w_lo_ready"], 2)
                    for n, (e0, e1) in enumerate(WB_PARTS):
                        if e1 == E:
                            wait(sp, "gw_done", T * CH + CH)
                        sp.dma_start(wb[:, e0:e1, :], w_dram[e0:e1, :].partition_broadcast(P)
                                     ).then_inc(S[f"wb_loaded{n}"], 16)

            walk(sp, step)
            sp.wait_ge(S["y_stored"], NT * 16)
            sp.wait_ge(S["x_loaded"], (NT + 1) * 16)
            sp.wait_ge(S["ctxc_loaded"], (NT // 2 + 1) * 32)

        @block.tensor
        def _(pe):
            def mm3(o, w_h, w_l, m_h, m_l, start=True, stop=True):
                nc.tensor.matmul(o, w_h, m_h, start=start, stop=False)
                nc.tensor.matmul(o, w_h, m_l, start=False, stop=False)
                return nc.tensor.matmul(o, w_l, m_h, start=False, stop=stop)

            pe.wait_ge(S["ident_ready"], 2)
            pe.wait_ge(S["attn_w_loaded"], 64)
            for q in range(HP):
                last = nc.tensor.transpose(gate_ps[0][:, q * P:(q + 1) * P],
                                           probs[:, 0, 2 * q:2 * q + 2, :].rearrange("p h j -> p (h j)"), ident[:, :])
            last.then_inc(S["prep_T"], 1)
            for q in range(HP):
                last = nc.tensor.transpose(gate_ps[1][:, q * CD:(q + 1) * CD],
                                           probs[0:CD, 1, 2 * q:2 * q + 2, :].rearrange("p h j -> p (h j)"),
                                           ident[0:CD, 0:CD])
            last.then_inc(S["prep_T"], 1)
            for q in range(HP):
                last = nc.tensor.transpose(up_ps[0][:, q * CD:(q + 1) * CD],
                                           probs[0:CD, 2, 2 * q:2 * q + 2, :].rearrange("p h j -> p (h j)"),
                                           ident[0:CD, 0:CD])
            last.then_inc(S["prep_T"], 1)
            pe.wait_ge(S["ctx_loaded"], 16)
            ctx_raw = x1[:, :, :, :].rearrange("p a k d -> p (a k d)")[:, 0:8 * CD].rearrange("p (s c) -> p s c", c=CD)
            for n in range(2):
                for s in range(4):
                    last = nc.tensor.transpose((up_ps[1], y_ps)[n][0:CD, s * P:(s + 1) * P], ctx_raw[:, 4 * n + s, :],
                                               ident[:, :])
                last.then_inc(S["prep_ctx_T"], 1)
            pe.wait_ge(S["small_loaded"], 64)
            nc.tensor.transpose(T_ps[:, 0:2 * CH], bgu_raw[:, :], ident[0:2 * CH, 0:2 * CH]).then_inc(S["bgu_T"], 1)
            pe.wait_ge(S["prep_T_read"], 3)
            wqT = y_out[:, :, :].rearrange("p k d -> p (k d)")
            for par in range(2):
                r = par * DH
                for q in range(HP):
                    last = nc.tensor.matmul((S_ps, O_ps)[par][0:CD, q * D:(q + 1) * D],
                                            ot_sb[r:r + DH, q * CD:(q + 1) * CD], wqT[r:r + DH, q * P:(q + 1) * P],
                                            start=True, stop=True)
                last.then_inc(S["prep_fold"], 1)
            for par in range(2):
                r = par * DH
                for q in range(HP):
                    last = nc.tensor.matmul(gate_ps[par][0:CD, q * D:(q + 1) * D],
                                            yT_sb[r:r + DH, q * CD:(q + 1) * CD],
                                            probs[r:r + DH, 3, 2 * q:2 * q + 2, :].rearrange("p h j -> p (h j)"),
                                            start=True, stop=True)
                last.then_inc(S["prep_fold"], 1)
            pe.wait_ge(S["prep_fold_lo"], 4)
            pe.wait_ge(S["bgu_ready"], 1)

            def a_piece(early, q, ps):
                for i in range(2):
                    h = 2 * q + i
                    last = mm3(ps[:, i * PAIR:(i + 1) * PAIR], m_hi[:, h, :], m_lo[:, h, :], ctxc_hi[:, :], ctxc_lo[:, :])
                last.then_inc(S["a_ready"], 1)

            def b_piece(odd_tile, q):
                w = slice(odd_tile * P, odd_tile * P + P)
                mm3(O_ps[:, :], ctxc_hi[:, w], ctxc_lo[:, w],
                    n_hi[:, 4 * q:4 * q + 4, :].rearrange("p h d -> p (h d)"),
                    n_lo[:, 4 * q:4 * q + 4, :].rearrange("p h d -> p (h d)")).then_inc(S["b_ready"], 1)

            def scores(early, odd_tile, k):
                b = odd_tile * BT + k // 2
                w = slice(k * P, k * P + P)
                mm3(S_ps[:, :], xnT_hi[:, w], xnT_lo[:, w], a_hi[:, b, :, :].rearrange("p h j -> p (h j)"),
                    a_lo[:, b, :, :].rearrange("p h j -> p (h j)")).then_inc(S["s_ready"], 1)

            def probs_T(a, k):
                pe.wait_ge(S["norm_done"], a * KT + k + 1)
                for q in range(HP):
                    last = nc.tensor.transpose(T_ps[:, q * P:(q + 1) * P],
                                               probs[:, k, 2 * q:2 * q + 2, :].rearrange("p h j -> p (h j)"),
                                               ident[:, :])
                last.then_inc(S["pT_ready"], 1)

            def attn_out(b):
                w = slice(b * SEQ, (b + 1) * SEQ)
                for q in range(HP):
                    last = mm3(O_ps[:, w], b_hi[:, b, q, :], b_lo[:, b, q, :], pT_hi[:, q, w], pT_lo[:, q, w],
                               start=(q == 0), stop=(q == HP - 1))
                last.then_inc(S["ot_ready"], 1)

            def step(T, c, odd):
                y_of, main, early = T - 1, T + 1, T + 2
                if live(T):
                    n = T * CH + c
                    rhs_h, rhs_l = xn2T_hi[:, odd, :], xn2T_lo[:, odd, :]
                    if c == 0:
                        pe.wait_ge(S["x2T_lo"], T + 1)
                    if c == 0 and isinstance(T, int) and T == 0:
                        pe.wait_ge(S["w_lo_ready"], 3)
                        pe.wait_ge(S["w_hi_ready"], 3)
                    wait(pe, "gate_done", n - 1)
                    mm3(gate_ps[c % 2][:, :], wg_hi[:, c, :], wg_lo[:, c, :], rhs_h, rhs_l).then_inc(S["gate_ready"], 1)
                    wait(pe, "h_done", n - 1)
                    mm3(up_ps[c % 2][:, :], wu_hi[:, c, :], wu_lo[:, c, :], rhs_h, rhs_l).then_inc(S["up_ready"], 1)
                t, d = (T, c - LAG) if c >= LAG else (T - 1, c - LAG + CH)
                if live(t):
                    if d == 0:
                        wait(pe, "y_read", t)
                        pe.wait_ge(S["wT_done"], t + 1)
                        if isinstance(t, int) and t == 0:
                            pe.wait_ge(S["bo_ready"], 32)
                        nc.tensor.matmul(y_ps[:, :], bo_hhl[:, :], wT_r[0:3 * E, :], start=True, stop=False)
                    pe.wait_ge(S["h_lo_done"], t * CH + d + 1)
                    mm3(y_ps[:, :], wo_hi[:, d, :], wo_lo[:, d, :], h_hi[:, d % NHB, :], h_lo[:, d % NHB, :],
                        start=False, stop=(d == CH - 1)).then_inc(S["down_done"], 1)

                if live(early):
                    if c in (5, 6) and not odd:
                        if c == 5:
                            pe.wait_ge(S["ctxc_loaded"], early * 16 + 32)
                            wait(pe, "ot_read", main * 2 + 2)
                            wait(pe, "s_sub", early * KT)
                        else:
                            pe.wait_ge(S["a_lo_done"], early * 2 + 2)
                        a_piece(early, 2 * (c - 5), O_ps)
                        a_piece(early, 2 * (c - 5) + 1, S_ps)
                    if c == 7:
                        pe.wait_ge(S["xn_ready"], early + 1)
                        wait(pe, "x1_ready", main * 2 + 2)
                        for k in range(KT):
                            last = nc.tensor.transpose(T_ps[:, k * P:(k + 1) * P], xn[:, k, :], ident[:, :])
                        last.then_inc(S["xT_ready"], 1)
                    if 8 <= c < 8 + KT:
                        k = c - 8
                        if k == 0:
                            pe.wait_ge(S["xT_lo"], early + 1)
                            pe.wait_ge(S["a_lo_done"], early * 2 + 4 if not odd else early * 2 + 2)
                        else:
                            pe.wait_ge(S["s_sub"], early * KT + k)
                        scores(early, odd, k)
                    if c in (8, 10):
                        q = (c - 8) // 2
                        if q == 0:
                            wait(pe, "ot_read", main * 2 + 2)
                        else:
                            pe.wait_ge(S["b_lo_done"], early * 2 + 1)
                        b_piece(odd, q)
                if c < 2 and live(main):
                    pe.wait_ge(S["pT_lo_done"], main * KT + c + 2)
                    probs_T(main, c + 2)
                if live(main):
                    if c == 2:
                        pe.wait_ge(S["b_moved"], main * 256 + 256)
                        pe.wait_ge(S["pT_lo_done"], main * KT + 2)
                        attn_out(0)
                    if c == 4:
                        pe.wait_ge(S["pT_lo_done"], main * KT + 4)
                        pe.wait_ge(S["ot_read"], main * 2 + 1)
                        attn_out(1)
                if c == 3 and live(y_of):
                    pe.wait_ge(S["y_read"], y_of + 1)
                    if live(main):
                        pe.wait_ge(S["pT_lo_done"], main * KT + 4)
                    for k in range(KT):
                        last = nc.tensor.transpose(T_ps[:, k * P:(k + 1) * P], yT_sb[:, k * P:(k + 1) * P], ident[:, :])
                    last.then_inc(S["yT_ready"], 1)
                if live(main):
                    if c in (4, 5):
                        b = c - 4
                        pe.wait_ge(S["ot_read"], main * 2 + b + 1)
                        if b == 0 and live(y_of):
                            pe.wait_ge(S["y_added"], y_of + 1)
                        if b == 1:
                            pe.wait_ge(S["x1_ready"], main * 2 + 1)
                        for k in (2 * b, 2 * b + 1):
                            last = nc.tensor.transpose(T_ps[:, k * P:(k + 1) * P], ot_sb[:, k * P:(k + 1) * P],
                                                       ident[:, :])
                        last.then_inc(S["ott_ready"], 1)
                    if c == 8:
                        if live(early):
                            pe.wait_ge(S["xT_lo"], early + 1)
                        pe.wait_ge(S["xn2_ready"], main + 1)
                        for k in range(KT):
                            last = nc.tensor.transpose(T_ps[:, k * P:(k + 1) * P], xn2[:, k, :], ident[:, :])
                        last.then_inc(S["x2T_ready"], 1)
                    if c == 11:
                        pe.wait_ge(S["x2T_lo"], main + 1)
                        if live(early):
                            pe.wait_ge(S["b_lo_done"], early * 2 + 2)
                        if isinstance(main, int) and main == 0:
                            pe.wait_ge(S["wr_ready"], 1)
                        for k in range(KT):
                            w = slice(k * P, k * P + P)
                            o = O_ps[:, 2 * E * k:2 * E * (k + 1)]
                            nc.tensor.matmul(o, xn2T_hi[:, 1 - odd, w], wr_hl[:, :, :].rearrange("p a e -> p (a e)"),
                                             start=True, stop=False)
                            last = nc.tensor.matmul(o[:, 0:E], xn2T_lo[:, 1 - odd, w], wr_hl[:, 0, :],
                                                    start=False, stop=True)
                        last.then_inc(S["router_ready"], 1)
                    if c == 13:
                        pe.wait_ge(S["w_ready"], main + 1)
                        for k in range(KT):
                            last = nc.tensor.transpose(T_ps[0:4 * E, k * P:(k + 1) * P], wst[:, k, :], ident[:, :])
                        last.then_inc(S["wT_ready"], 1)
                if c >= 14 and live(early):
                    if c == 14 and live(main):
                        pe.wait_ge(S["wT_done"], main + 1)
                    if c == 15:
                        pe.wait_ge(S["pT_lo_done"], early * KT + 1)
                    probs_T(early, c - 14)

            walk(pe, step)

        @block.scalar
        def _(act):
            copy = nc.scalar.copy
            act.wait_ge(S["prep_T"], 1)
            copy(y_out[:, :, :].rearrange("p k d -> p (k d)"), gate_ps[0][:, :]).then_inc(S["prep_T_read"], 1)
            act.wait_ge(S["prep_T"], 2)
            copy(ot_sb[:, 0:HP * CD], gate_ps[1][:, 0:HP * CD]).then_inc(S["prep_T_read"], 1)
            act.wait_ge(S["prep_T"], 3)
            copy(yT_sb[:, 0:HP * CD], up_ps[0][:, 0:HP * CD]).then_inc(S["prep_T_read"], 1)
            for n in range(2):
                act.wait_ge(S["prep_ctx_T"], n + 1)
                copy(ctxT_hi[:, n * 512:(n + 1) * 512], (up_ps[1], y_ps)[n][0:CD, :]).then_inc(S["prep_ctx_hi"], 1)
            act.wait_ge(S["bgu_T"], 1)
            copy(bgu[:, :, :].rearrange("p a c -> p (a c)"), T_ps[:, 0:2 * CH]).then_inc(S["bgu_ready"], 1)
            for n in range(4):
                act.wait_ge(S["prep_fold"], n + 1)
                dst = (m_hi, m_hi, n_hi, n_hi)[n][:, :, :].rearrange("p (q r) d -> p r q d", r=2)[:, n % 2, :, :]
                nc.scalar.mul(dst, folded(n),
                              SCALE if n < 2 else 1.0).then_inc(S["prep_fold_hi"], 1)
            act.wait_ge(S["small_loaded"], 64)
            copy(wr_hl[:, 0, :], wr_raw[:, :]).then_inc(S["wr_hi_ready"], 1)
            act.wait_ge(S["bo_loaded"], 48)
            copy(bo_hi[:, :], bo_raw[:, :]).then_inc(S["bo_hi_ready"], 1)

            def step(T, c, odd):
                y_of, main, early = T - 1, T + 1, T + 2
                if c == 3 and live(y_of):
                    act.wait_ge(S["down_done"], y_of * CH + CH)
                    copy(yT_sb[:, :], y_ps[:, :]).then_inc(S["y_read"], 1)
                if live(T):
                    n = T * CH + c
                    act.wait_ge(S["gate_ready"], n + 1)
                    wait(act, "gw_done", n - 1)
                    nc.scalar.activation(gate_sb(c), gate_ps[c % 2][:, :], ACT.Silu, bias=bgu[:, 0, c:c + 1]
                                         ).then_inc(S["gate_done"], 1)
                t, d = (T, c - 1) if c >= 1 else (T - 1, CH - 1)
                if live(t):
                    act.wait_ge(S["h_done"], t * CH + d + 1)
                    wait(act, "down_done", t * CH + d - NHB + 1)
                    copy(h_hi[:, d % NHB, :], h_sb(d)).then_inc(S["h_hi_done"], 1)
                if isinstance(T, int) and T == -1 and 2 <= c < 5:
                    if c == 2:
                        act.wait_ge(S["ffn_w_loaded"], 48)
                    w, src = ((wg_hi, wb[:, 0:4, :]), (wu_hi, wb[:, 4:8, :]), (wo_hi, ffn_tmp[:, 0:4, :]))[c - 2]
                    copy(w[:, :, :].rearrange("p c n -> p (c n)"), src.rearrange("p a n -> p (a n)")
                         ).then_inc(S["w_hi_ready"], 1)
                if live(main) and c == 7:
                    act.wait_ge(S["ln2_rstd"], main + 1)
                    for k in range(KT):
                        last = nc.scalar.activation(xn2[:, k, :], x1[:, 1 - odd, k, :], ACT.Identity,
                                                    bias=nmr[:, KT + k:KT + k + 1], scale=rstd[:, KT + k:KT + k + 1])
                    last.then_inc(S["xn2_ready"], 1)
                if live(early):
                    if c == 6:
                        act.wait_ge(S["ln1_rstd"], early + 1)
                        act.wait_ge(S["x_loaded"], early * 16 + 16)
                        for k in range(KT):
                            last = nc.scalar.activation(xn[:, k, :], x_raw[:, odd, k, :], ACT.Identity,
                                                        bias=nmr[:, k:k + 1], scale=rstd[:, k:k + 1])
                        last.then_inc(S["xn_ready"], 1)
                    if c in (5, 6) and not odd:
                        for i in range(2):
                            q = 2 * (c - 5) + i
                            act.wait_ge(S["a_ready"], early * 2 + q + 1)
                            copy(a_hi[:, :, 2 * q:2 * q + 2, :].rearrange("p b h j -> p h b j"),
                                 (O_ps, S_ps)[i][:, :].rearrange("p (h b j) -> p h b j", h=2, j=J)
                                 ).then_inc(S["a_hi_done"], 1)
                    if c == 7:
                        act.wait_ge(S["xT_ready"], early + 1)
                        copy(xnT_hi[:, :], T_ps[:, :]).then_inc(S["xT_hi"], 1)
                    if c in (8, 10):
                        q = (c - 8) // 2
                        act.wait_ge(S["b_ready"], early * 2 + q + 1)
                        wait(act, "b_moved", early * 256)
                        copy(bs_hi[:, 4 * q:4 * q + 4, :].rearrange("p h d -> p (h d)"), O_ps[:, :]
                             ).then_inc(S["b_hi_done"], 1)
                if live(main):
                    if c == 12:
                        act.wait_ge(S["logits_ready"], main + 1)
                        nc.scalar.activation(lg_e[:, :, :], lg_d[:, :, :], ACT.Exp).then_inc(S["route_exp"], 1)
                if live(early):
                    if c == 12:
                        act.wait_ge(S["s_sub"], early * KT + KT)
                        for i in range(2):
                            last = nc.scalar.activation(probs[:, 2 * i:2 * i + 2, :, :], probs[:, 2 * i:2 * i + 2, :, :],
                                                        ACT.Exp)
                            last.then_inc(S["exp_done"], 1)
                for a, k, on in ((early, c - 14, c >= 14), (main, c + 2, c < 2)):
                    if on and live(a):
                        act.wait_ge(S["pT_ready"], a * KT + k + 1)
                        copy(pT_hi[:, :, k * P:(k + 1) * P], T_ps[:, :].rearrange("p (q n) -> p q n", q=HP)
                             ).then_inc(S["pT_hi_done"], 1)
                if live(main):
                    if c in (2, 4):
                        b = (c - 2) // 2
                        act.wait_ge(S["ot_ready"], main * 2 + b + 1)
                        nc.scalar.activation(ot_sb[:, b * SEQ:(b + 1) * SEQ], O_ps[:, b * SEQ:(b + 1) * SEQ], ACT.Identity,
                                             bias=bout_col[:, 0:1]).then_inc(S["ot_read"], 1)
                    if c == 8:
                        act.wait_ge(S["x2T_ready"], main + 1)
                        copy(xn2T_hi[:, 1 - odd, :], T_ps[:, :]).then_inc(S["x2T_hi"], 1)

            walk(act, step)

        @block.gpsimd
        def _(pool):
            nc.gpsimd.memset(ident[:, :], 0.0).then_inc(S["ident_ready"], 1)
            pool.wait_ge(S["ident_ready"], 1)
            nc.gpsimd.affine_select(out=ident[:, :], in_=ident[:, :], compare_op=ALU.not_equal, fill=1.0, base=0,
                                    pattern=[[-1, P]], channel_multiplier=1).then_inc(S["ident_ready"], 1)
            nc.gpsimd.memset(m_half[:, :], -0.5).then_inc(S["half_ready"], 1)
            nc.gpsimd.iota(iota_e[:, :, :], [[0, KT], [1, E]], base=0, channel_multiplier=0,
                           allow_small_or_imprecise_dtypes=True).then_inc(S["iota_ready"], 1)
            pool.wait_ge(S["small_loaded"], 64)
            pool.wait_ge(S["half_ready"], 1)

            def step(T, c, odd):
                main, early = T + 1, T + 2
                if live(T):
                    n = T * CH + c
                    for part, (e0, _) in enumerate(WB_PARTS):
                        if c == e0 * MC:
                            pool.wait_ge(S[f"wb_loaded{part}"], T * 16 + 16)
                    pool.wait_ge(S["gate_done"], n + 1)
                    wait(pool, "h_done", n - 1)
                    nc.gpsimd.tensor_tensor(gw_sb(c), gate_sb(c), wb[:, c // MC, :], ALU.mult).then_inc(S["gw_done"], 1)
                if live(early):
                    if c == 5:
                        pool.wait_ge(S["ln1_stats"], early * 4 + 4)
                        nc.gpsimd.tensor_tensor(rstd[:, 0:KT], var_eps[:, 0:KT], m_half[:, 0:KT], ALU.pow
                                                ).then_inc(S["ln1_pow"], 1)
                        pool.wait_ge(S["ln1_pow"], early + 1)
                        nc.gpsimd.tensor_tensor(nmr[:, 0:KT], neg_mean[:, 0:KT], rstd[:, 0:KT], ALU.mult
                                                ).then_inc(S["ln1_rstd"], 1)
                    if c in (13, 14, 15):
                        norm(early, c - 13)
                if live(main):
                    if c == 0:
                        norm(main, 3)
                    if c == 6:
                        w = slice(KT, 2 * KT)
                        pool.wait_ge(S["ln2_stats"], main * 4 + 4)
                        nc.gpsimd.tensor_tensor(rstd[:, w], var_eps[:, w], m_half[:, w], ALU.pow
                                                ).then_inc(S["ln2_pow"], 1)
                        pool.wait_ge(S["ln2_pow"], main + 1)
                        nc.gpsimd.tensor_tensor(nmr[:, w], neg_mean[:, w], rstd[:, w], ALU.mult
                                                ).then_inc(S["ln2_rstd"], 1)

            def norm(a, k):
                pool.wait_ge(S["inv_done"], a * 2 + k // 2 + 1)
                nc.gpsimd.tensor_tensor(probs[:, k, :, :], probs[:, k, :, :],
                                        r_inv[:, k, :].unsqueeze(2).to_broadcast([P, H, J]), ALU.mult
                                        ).then_inc(S["norm_done"], 1)

            walk(pool, step)

        @block.vector
        def _(dve):
            V = nc.vector

            for n in range(2):
                dve.wait_ge(S["prep_ctx_hi"], n + 1)
                w = slice(n * 512, (n + 1) * 512)
                V.tensor_tensor(ctxT_lo[:, w], (up_ps[1], y_ps)[n][0:CD, :], as_f32(ctxT_hi[:, w]), ALU.subtract
                                ).then_inc(S["prep_ctx_lo"], 1)
            for n in range(4):
                dve.wait_ge(S["prep_fold_hi"], n + 1)
                hi, lo = ((m_hi, m_lo), (m_hi, m_lo), (n_hi, n_lo), (n_hi, n_lo))[n]
                hi, lo = (w[:, :, :].rearrange("p (q r) d -> p r q d", r=2)[:, n % 2, :, :] for w in (hi, lo))
                V.scalar_tensor_tensor(lo, folded(n), SCALE if n < 2 else 1.0, as_f32(hi), ALU.mult, ALU.subtract
                                       ).then_inc(S["prep_fold_lo"], 1)
            dve.wait_ge(S["wr_hi_ready"], 1)
            V.tensor_tensor(wr_hl[:, 1, :], wr_raw[:, :], as_f32(wr_hl[:, 0, :]), ALU.subtract).then_inc(S["wr_ready"], 1)
            dve.wait_ge(S["bo_hi_ready"], 1)
            V.tensor_tensor(bo_lo[:, :], bo_raw[:, :], as_f32(bo_hi[:, :]), ALU.subtract).then_inc(S["bo_lo_ready"], 1)
            dve.wait_ge(S["iota_ready"], 1)
            dve.wait_ge(S["bgu_ready"], 1)

            def stats(src, col, ks, base, name):
                for k in ks:
                    last = V.bn_stats(bn[:, col + k, :], src(k))
                last.then_inc(S[name], 1)
                w = slice(col + ks[0], col + ks[-1] + 1)
                dve.wait_ge(S[name], base + 1)
                V.tensor_tensor(m_diff[:, w], bn[:, w, 1], bn[:, w, 4], ALU.subtract)
                V.tensor_tensor(v_sum[:, w], bn[:, w, 2], bn[:, w, 5], ALU.add).then_inc(S[name], 1)
                dve.wait_ge(S[name], base + 2)
                V.scalar_tensor_tensor(m_sq[:, w], m_diff[:, w], 0.25, m_diff[:, w], ALU.mult, ALU.mult)
                V.tensor_scalar(v_eps[:, w], v_sum[:, w], 1.0 / D, EPS, ALU.mult, ALU.add)
                V.scalar_tensor_tensor(neg_mean[:, w], m_diff[:, w], -0.5, bn[:, w, 4], ALU.mult, ALU.subtract
                                       ).then_inc(S[name], 1)
                dve.wait_ge(S[name], base + 3)
                V.tensor_tensor(var_eps[:, w], v_eps[:, w], m_sq[:, w], ALU.add).then_inc(S[name], 1)

            def split_lo(lo, full, hi):
                return V.tensor_tensor(lo, full, as_f32(hi), ALU.subtract)

            ROUTE = 8

            def step(T, c, odd):
                y_of, main, early = T - 1, T + 1, T + 2
                if isinstance(T, int) and T == -1 and 2 <= c < 5:
                    dve.wait_ge(S["w_hi_ready"], c - 1)
                    hi, lo, src = ((wg_hi, wg_lo, wb[:, 0:4, :]), (wu_hi, wu_lo, wb[:, 4:8, :]),
                                   (wo_hi, wo_lo, ffn_tmp[:, 0:4, :]))[c - 2]
                    split_lo(lo[:, :, :].rearrange("p c n -> p (c n)"), src.rearrange("p a n -> p (a n)"),
                             hi[:, :, :].rearrange("p c n -> p (c n)")).then_inc(S["w_lo_ready"], 1)

                for a, k, on in ((early, 0, c == 15), (main, c + 1, c < 3)):
                    if on and live(a):
                        dve.wait_ge(S["pT_hi_done"], a * KT + k + 1)
                        split_lo(pT_lo[:, :, k * P:(k + 1) * P], T_ps[:, :].rearrange("p (q n) -> p q n", q=HP),
                                 pT_hi[:, :, k * P:(k + 1) * P]).then_inc(S["pT_lo_done"], 1)
                if c == 4 and live(y_of):
                    dve.wait_ge(S["yT_ready"], y_of + 1)
                    V.tensor_tensor(y_out[:, :, :].rearrange("p k d -> p (k d)"), T_ps[:, :],
                                    x1[:, 1 - odd, :, :].rearrange("p k d -> p (k d)"), ALU.add).then_inc(S["y_added"], 1)
                if live(main):
                    if c in (5, 6):
                        b = c - 5
                        dve.wait_ge(S["ott_ready"], main * 2 + b + 1)
                        dve.wait_ge(S["x_loaded"], main * 16 + 16)
                        V.tensor_tensor(x1[:, 1 - odd, 2 * b:2 * b + 2, :],
                                        T_ps[:, b * SEQ:(b + 1) * SEQ].rearrange("p (k d) -> p k d", d=D),
                                        x_raw[:, 1 - odd, 2 * b:2 * b + 2, :], ALU.add).then_inc(S["x1_ready"], 1)
                if live(early):
                    if c == 8:
                        dve.wait_ge(S["xT_hi"], early + 1)
                        split_lo(xnT_lo[:, :], T_ps[:, :], xnT_hi[:, :]).then_inc(S["xT_lo"], 1)
                    if c in (6, 7) and not odd:
                        for i in range(2):
                            q = 2 * (c - 6) + i
                            dve.wait_ge(S["a_hi_done"], early * 2 + q + 1)
                            w = (slice(None), slice(None), slice(2 * q, 2 * q + 2), slice(None))
                            split_lo(a_lo[w].rearrange("p b h j -> p h b j"),
                                     (O_ps, S_ps)[i][:, :].rearrange("p (h b j) -> p h b j", h=2, j=J),
                                     a_hi[w].rearrange("p b h j -> p h b j")).then_inc(S["a_lo_done"], 1)
                    if 9 <= c < 9 + KT:
                        k = c - 9
                        s3 = S_ps[:, :].rearrange("p (h j) -> p h j", h=H)
                        dve.wait_ge(S["s_ready"], early * KT + k + 1)
                        V.tensor_reduce(s_max[:, k, :], s3, AX_X, ALU.max).then_inc(S["s_maxed"], 1)
                        dve.wait_ge(S["s_maxed"], early * KT + k + 1)
                        V.tensor_tensor(probs[:, k, :, :], s3, s_max[:, k, :].unsqueeze(2).to_broadcast([P, H, J]),
                                        ALU.subtract).then_inc(S["s_sub"], 1)
                if live(main) and c == 9:
                    dve.wait_ge(S["x2T_hi"], main + 1)
                    split_lo(xn2T_lo[:, 1 - odd, :], T_ps[:, :], xn2T_hi[:, 1 - odd, :]).then_inc(S["x2T_lo"], 1)
                if live(early) and c in (9, 11):
                    q = (c - 9) // 2
                    dve.wait_ge(S["b_hi_done"], early * 2 + q + 1)
                    w = slice(4 * q, 4 * q + 4)
                    split_lo(bs_lo[:, w, :].rearrange("p h d -> p (h d)"), O_ps[:, :],
                             bs_hi[:, w, :].rearrange("p h d -> p (h d)")).then_inc(S["b_lo_done"], 1)
                if live(main) and c == 12:
                    at = main * ROUTE
                    o = O_ps[:, 0:KT * 2 * E].rearrange("p (k a e) -> p k a e", k=KT, a=2)
                    dve.wait_ge(S["router_ready"], main + 1)
                    V.tensor_copy(lg_lo[:, :, :], o[:, :, 1, :]).then_inc(S["route_step"], 1)
                    dve.wait_ge(S["route_step"], at + 1)
                    V.tensor_tensor(lg[:, :, :], o[:, :, 0, :], lg_lo[:, :, :], ALU.add).then_inc(S["route_step"], 1)
                    dve.wait_ge(S["route_step"], at + 2)
                    V.tensor_copy(lg_lo[:, :, :], lg[:, :, :])
                    for k in range(KT):
                        last = V.max(top[:, k, :], lg[:, k, :])
                    last.then_inc(S["route_step"], 1)
                    dve.wait_ge(S["route_step"], at + 3)
                    V.tensor_tensor(lg_d[:, :, :], lg[:, :, :], top[:, :, 0:1].to_broadcast([P, KT, E]), ALU.subtract
                                    ).then_inc(S["logits_ready"], 1)
                if live(main) and c == 13:
                    at = main * ROUTE
                    dve.wait_ge(S["route_exp"], main + 1)
                    dve.wait_ge(S["route_step"], at + 6)
                    V.tensor_tensor(sel_e[:, :, :], sel[:, :, :], lg_e[:, :, :], ALU.mult)
                    V.tensor_reduce(den_a[:, :], lg_e[:, :, :], AX_X, ALU.add).then_inc(S["route_step"], 1)
                    dve.wait_ge(S["route_step"], at + 7)
                    V.tensor_reduce(den_b[:, :], sel_e[:, :, :], AX_X, ALU.add).then_inc(S["route_step"], 1)
                    dve.wait_ge(S["route_step"], at + 8)
                    V.scalar_tensor_tensor(den[:, :], den_a[:, :], NORM_EPS, den_b[:, :], ALU.mult, ALU.add
                                           ).then_inc(S["w_steps"], 1)
                    dve.wait_ge(S["w_steps"], main * 3 + 1)
                    V.reciprocal(den_inv[:, :], den[:, :]).then_inc(S["w_steps"], 1)
                    dve.wait_ge(S["w_steps"], main * 3 + 2)
                    V.tensor_tensor(wst[:, :, 3 * E:4 * E], sel_e[:, :, :],
                                    den_inv[:, :].unsqueeze(2).to_broadcast([P, KT, E]), ALU.mult)
                    V.tensor_tensor(wst[:, :, 0:E].bitcast(F32R), sel_e[:, :, :],
                                    den_inv[:, :].unsqueeze(2).to_broadcast([P, KT, E]), ALU.mult)
                    V.tensor_tensor(wst[:, :, 2 * E:3 * E].bitcast(F32R), sel_e[:, :, :],
                                    den_inv[:, :].unsqueeze(2).to_broadcast([P, KT, E]), ALU.mult
                                    ).then_inc(S["w_steps"], 1)
                    dve.wait_ge(S["w_steps"], main * 3 + 3)
                    V.tensor_tensor(wst[:, :, E:2 * E], wst[:, :, 3 * E:4 * E], wst[:, :, 0:E], ALU.subtract
                                    ).then_inc(S["w_ready"], 1)
                if live(y_of) and c == 14:
                    dve.wait_ge(S["y_stored"], y_of * 16 + 16)
                if live(main) and c == 14:
                    dve.wait_ge(S["wT_ready"], main + 1)
                    wait(dve, "w_saved", main * 16)
                    V.tensor_copy(wT[:, :], T_ps[0:4 * E, :])
                    V.tensor_copy(wT_r[:, :], T_ps[0:4 * E, :]).then_inc(S["wT_done"], 1)
                t, d = (T, c - 1) if c >= 1 else (T - 1, c - 1 + CH)
                if live(t):
                    dve.wait_ge(S["gw_done"], t * CH + d + 1)
                    dve.wait_ge(S["up_ready"], t * CH + d + 1)
                    wait(dve, "h_lo_done", t * CH + d - 1)
                    V.scalar_tensor_tensor(h_sb(d), up_ps[d % 2][:, :], bgu[:, 1, d:d + 1], gw_sb(d), ALU.add, ALU.mult
                                           ).then_inc(S["h_done"], 1)
                t, d = (T, c - 2) if c >= 2 else (T - 1, c - 2 + CH)
                if live(t):
                    dve.wait_ge(S["h_hi_done"], t * CH + d + 1)
                    split_lo(h_lo[:, d % NHB, :], h_sb(d), h_hi[:, d % NHB, :]).then_inc(S["h_lo_done"], 1)
                if live(early) and c == 5:
                    dve.wait_ge(S["x_loaded"], early * 16 + 16)
                    wait(dve, "ln1_rstd", early)
                    stats(lambda k: x_raw[:, odd, k, :], 0, range(KT), early * 4, "ln1_stats")
                if live(main) and c == 6:
                    dve.wait_ge(S["x1_ready"], main * 2 + 2)
                    stats(lambda k: x1[:, 1 - odd, k, :], KT, range(KT), main * 4, "ln2_stats")
                if live(main) and c == 12:
                    at = main * ROUTE
                    for k in range(KT):
                        last = V.max_index(top_at[:, k, :], top[:, k, :], lg[:, k, :])
                    last.then_inc(S["route_step"], 1)
                    dve.wait_ge(S["route_step"], at + 4)
                    V.tensor_tensor(oh1[:, :, :], iota_e[:, :, :], top_at[:, :, 0:1].to_broadcast([P, KT, E]),
                                    ALU.is_equal)
                    V.tensor_tensor(oh2[:, :, :], iota_e[:, :, :], top_at[:, :, 1:2].to_broadcast([P, KT, E]),
                                    ALU.is_equal).then_inc(S["route_step"], 1)
                    dve.wait_ge(S["route_step"], at + 5)
                    V.tensor_tensor(sel[:, :, :], oh1[:, :, :], oh2[:, :, :], ALU.add).then_inc(S["route_step"], 1)
                if live(early) and c in (13, 14):
                    i = c - 13
                    w = slice(2 * i, 2 * i + 2)
                    dve.wait_ge(S["exp_done"], early * 2 + i + 1)
                    V.tensor_reduce(r_sum[:, w, :], probs[:, w, :, :], AX_X, ALU.add).then_inc(S["sums_done"], 1)
                    dve.wait_ge(S["sums_done"], early * 2 + i + 1)
                    V.reciprocal(r_inv[:, w, :], r_sum[:, w, :]).then_inc(S["inv_done"], 1)

            walk(dve, step)


_INS = ['x', 'ctx_768', 'L0_xattn_Wq', 'L0_xattn_Wk', 'L0_xattn_Wv', 'L0_xattn_Wout', 'L0_xattn_bout',
        'L0_ffn_W_router', 'L0_ffn_W_gate', 'L0_ffn_b_gate', 'L0_ffn_W_up', 'L0_ffn_b_up', 'L0_ffn_W_out',
        'L0_ffn_b_out']
_OUTS = [((16, 256, 128), 'float32')]


def kernel(**inputs):
    import numpy as _np
    import concourse.bacc as _bacc
    from concourse import mybir as _mybir
    from concourse.bass_utils import run_bass_kernel_spmd as _run

    nc = _bacc.Bacc("TRN2", target_bir_lowering=False, num_devices=1)
    arrays, args = {}, []
    for name in _INS:
        a = _np.ascontiguousarray(inputs[name])
        arrays[f"in_{name}_dram"] = a
        args.append(nc.dram_tensor(f"in_{name}_dram", a.shape, _mybir.dt.from_np(a.dtype), kind="ExternalInput").ap())
    for i, (shape, dtype) in enumerate(_OUTS):
        dt = _mybir.dt.from_np(_np.dtype(dtype))
        args.append(nc.dram_tensor(f"out_{i}_dram", shape, dt, kind="ExternalOutput").ap())
    xattn_moe_kernel(nc, *args)
    r = _run(nc, [arrays], core_ids=[0])
    got = tuple(r.results[0][f"out_{i}_dram"] for i in range(len(_OUTS)))
    return got[0]
```

```python
from contextlib import ExitStack

import concourse.bass as bass
from concourse import mybir

F32 = mybir.dt.float32
F32R = mybir.dt.float32r
U32 = mybir.dt.uint32
ALU = mybir.AluOpType
ACT = mybir.ActivationFunctionType
AX_X = mybir.AxisListType.X

P = 128
EPS = 1e-5
NORM_EPS = 1e-8


def xattn_moe_kernel(nc, x, ctx_in, Wq, Wk, Wv, Wout, bout, Wr, Wg, bg, Wu, bu, Wo, bo, out):
    NB, SEQ, D = x.shape
    _, J, CD = ctx_in.shape
    INNER = Wq.shape[1]
    DH = 64
    H = INNER // DH
    HP = H // 2
    E, _, M = Wg.shape
    MC = M // P
    TOK = 512
    KT = TOK // P
    BT = TOK // SEQ
    NT = NB * SEQ // TOK
    CH = E * MC
    HB = H // 2
    SCALE = DH ** -0.5
    LAG = 3
    WB_PARTS = ((0, 2), (2, 6), (6, 8))
    NHB = 4
    PAIR = 2 * BT * J
    assert D == P and CH == 16 and J * 2 == P and TOK == 512 and NT % 2 == 0 and E == 8 and BT == 2

    x_t = x.rearrange("(t b) (s p) d -> t p (b s) d", b=BT, p=P)
    out_t = out.rearrange("(t b) (s p) d -> t p (b s) d", b=BT, p=P)
    ctxT_dram = [nc.dram_tensor(f"ctxT_{n}_scratch", (CD, (NT + 1) * BT * J), F32, kind="Internal").ap() for n in ("hi", "lo")]
    w_dram = nc.dram_tensor("expert_weights_scratch", (E, TOK), F32, kind="Internal").ap()

    with ExitStack() as stack:
        def sb(name, shape, dt=F32):
            return stack.enter_context(nc.sbuf_tensor(name, shape, dt))

        def sem(name):
            return stack.enter_context(nc.semaphore(name))

        ident = sb("ident", [P, P])
        wg_hi = sb("wg_hi", [P, CH, P], F32R)
        wg_lo = sb("wg_lo", [P, CH, P], F32R)
        wu_hi = sb("wu_hi", [P, CH, P], F32R)
        wu_lo = sb("wu_lo", [P, CH, P], F32R)
        wo_hi = sb("wo_hi", [P, CH, D], F32R)
        wo_lo = sb("wo_lo", [P, CH, D], F32R)
        m_hi = sb("m_hi", [CD, H, D], F32R)
        m_lo = sb("m_lo", [CD, H, D], F32R)
        n_hi = sb("n_hi", [CD, H, D], F32R)
        n_lo = sb("n_lo", [CD, H, D], F32R)
        wr_raw = sb("wr_raw", [P, E])
        wr_hl = sb("wr_hl", [P, 2, E], F32R)
        bout_col = sb("bout_col", [D, 1])
        bgu_raw = sb("bgu_raw", [2 * CH, P])
        bgu = sb("bgu", [P, 2, CH])
        bo_raw = sb("bo_raw", [3 * E, D])
        bo_hi = sb("bo_hi", [3 * E, D], F32R)
        bo_lo = sb("bo_lo", [3 * E, D], F32R)
        bo_hhl = sb("bo_hhl", [3 * E, D], F32R)
        iota_e = sb("iota_e", [P, KT, E])

        x_raw = sb("x_raw", [P, 2, KT, D])
        bn = sb("bn", [P, 2 * KT, 6])
        m_diff = sb("m_diff", [P, 2 * KT])
        m_sq = sb("m_sq", [P, 2 * KT])
        v_sum = sb("v_sum", [P, 2 * KT])
        v_eps = sb("v_eps", [P, 2 * KT])
        var_eps = sb("var_eps", [P, 2 * KT])
        neg_mean = sb("neg_mean", [P, 2 * KT])
        rstd = sb("rstd", [P, 2 * KT])
        nmr = sb("nmr", [P, 2 * KT])
        m_half = sb("m_half", [P, 2 * KT])
        xn = sb("xn", [P, KT, D])
        xnT_hi = sb("xnT_hi", [P, TOK], F32R)
        xnT_lo = sb("xnT_lo", [P, TOK], F32R)
        ctxc_hi = sb("ctxc_hi", [CD, PAIR], F32R)
        ctxc_lo = sb("ctxc_lo", [CD, PAIR], F32R)
        a_hi = sb("a_hi", [P, 2 * BT, H, J], F32R)
        a_lo = sb("a_lo", [P, 2 * BT, H, J], F32R)
        bs_hi = sb("bs_hi", [P, H, D], F32R)
        bs_lo = sb("bs_lo", [P, H, D], F32R)
        b_hi = sb("b_hi", [P, BT, HP, D], F32R)
        b_lo = sb("b_lo", [P, BT, HP, D], F32R)
        s_max = sb("s_max", [P, KT, H])
        probs = sb("probs", [P, KT, H, J])
        r_sum = sb("r_sum", [P, KT, H])
        r_inv = sb("r_inv", [P, KT, H])
        pT_hi = sb("pT_hi", [P, HP, TOK], F32R)
        pT_lo = sb("pT_lo", [P, HP, TOK], F32R)
        ctxT_hi = pT_hi[0:CD, :, :].rearrange("p q n -> p (q n)")[:, 0:NB * J]
        ctxT_lo = pT_lo[0:CD, :, :].rearrange("p q n -> p (q n)")[:, 0:NB * J]
        ot_sb = sb("ot_sb", [P, TOK])
        x1 = sb("x1", [P, 2, KT, D])
        xn2 = sb("xn2", [P, KT, D])
        xn2T_hi = sb("xn2T_hi", [P, 2, TOK], F32R)
        xn2T_lo = sb("xn2T_lo", [P, 2, TOK], F32R)

        lg_lo = sb("lg_lo", [P, KT, E])
        lg = sb("lg", [P, KT, E])
        top = sb("top", [P, KT, 8])
        top_at = sb("top_at", [P, KT, 8], U32)
        lg_d = sb("lg_d", [P, KT, E])
        lg_e = sb("lg_e", [P, KT, E])
        oh1 = sb("oh1", [P, KT, E])
        oh2 = sb("oh2", [P, KT, E])
        sel = sb("sel", [P, KT, E])
        sel_e = sb("sel_e", [P, KT, E])
        den_a = sb("den_a", [P, KT])
        den_b = sb("den_b", [P, KT])
        den = sb("den", [P, KT])
        den_inv = sb("den_inv", [P, KT])
        wst = sb("wst", [P, KT, 4 * E])
        wT = sb("wT", [4 * E, TOK])
        wT_r = sb("wT_r", [4 * E, TOK], F32R)
        wb = sb("wb", [P, E, TOK])

        ffn_tmp = sb("ffn_tmp", [P, 6, TOK])
        h_hi = sb("h_hi", [P, NHB, TOK], F32R)
        h_lo = sb("h_lo", [P, NHB, TOK], F32R)
        yT_sb = sb("yT_sb", [P, TOK])
        y_out = sb("y_out", [P, KT, D])

        def gate_sb(c):
            return ffn_tmp[:, c % 2, :]

        def gw_sb(c):
            return ffn_tmp[:, 2 + c % 2, :]

        def h_sb(c):
            return ffn_tmp[:, 4 + c % 2, :]

        def bank(name):
            return stack.enter_context(nc.psum_tensor(name, [P, 512], F32))

        gate_ps = [bank("gate_ps0"), bank("gate_ps1")]
        up_ps = [bank("up_ps0"), bank("up_ps1")]
        y_ps = bank("y_ps")
        T_ps = bank("T_ps")
        S_ps = bank("S_ps")
        O_ps = bank("O_ps")

        names = (
            "x_loaded wq_loaded wk_loaded wv_loaded wout_loaded ctx_loaded small_loaded ffn_w_loaded bo_loaded ident_ready prep_T wqT_read wkT_read wvT_read "
            "prep_ctx_T prep_ctx_hi prep_ctx_lo ctxc_lo_done prep_fold prep_fold_hi prep_fold_lo ctxT_saved ctxc_loaded bgu_T bgu_ready "
            "w_hi_ready w_lo_ready wr_hi_ready wr_ready bo_hi_ready bo_lo_ready bo_ready iota_ready half_ready "
            "ln1_stats ln1_pow ln1_rstd xn_ready xT_ready xT_hi xT_lo "
            "a_ready a_hi_done a_lo_done b_ready b_hi_done b_lo_done b_moved "
            "s_ready s_maxed s_sub exp_done sums_done inv_done norm_done pT_ready pT_hi_done pT_lo_done "
            "ot_ready ot_read ott_ready x1_ready ln2_stats ln2_pow ln2_rstd xn2_ready "
            "x2T_ready x2T_hi x2T_lo router_ready route_step w_steps logits_ready route_exp w_ready wT_ready wT_done "
            "w_saved wb_loaded0 wb_loaded1 wb_loaded2 "
            "gate_ready gate_done gw_done up_ready h_done h_hi_done h_lo_done down_done "
            "y_read yT_ready y_added y_stored"
        ).split()
        S = {n: sem(n) for n in names}

        def wait(eng, name, value):
            if not isinstance(value, int) or value > 0:
                eng.wait_ge(S[name], value)

        def live(t):
            return t is not None and (not isinstance(t, int) or 0 <= t < NT)

        def first(t):
            return isinstance(t, int) and t == 0

        def prologue(t):
            return isinstance(t, int) and t < 2

        def ahead(t):
            return t if isinstance(t, int) else t % NT

        def walk(eng, step):
            for half, c in PROLOGUE:
                if half == 0:
                    step(-2, c, 0)
                elif half == 1:
                    step(-1, c, 1, early_on=False)
                else:
                    step(-1, c, 1, main_on=False)
            for c in range(5):
                step(0, c, 0)
            with eng.Fori(0, NT // 2 - 1) as pair:
                T = pair * 2
                for c in range(5, CH):
                    step(T, c, 0)
                for c in range(CH):
                    step(T + 1, c, 1)
                for c in range(5):
                    step(T + 2, c, 0)
            for c in range(5, CH):
                step(NT - 2, c, 0)
            for c in range(CH):
                step(NT - 1, c, 1)
            for c in range(5):
                step(NT, c, 0)

        PROLOGUE = (*((0, c) for c in range(5, 13)), (2, 5), (2, 6), (2, 7), (0, 13), (0, 14), (0, 15),
                    *((1, c) for c in range(7)), (2, 8), (2, 9), (1, 7), (2, 10), (2, 11), (1, 8), (2, 12),
                    (1, 9), (1, 10), (1, 11), (2, 13), (1, 12), (1, 13), (2, 14), (1, 14), (1, 15), (2, 15))

        def as_f32(ap):
            return ap.bitcast(F32)

        def folded(n):
            return (S_ps, O_ps, gate_ps[0], gate_ps[1])[n][0:CD, :].rearrange("p (q d) -> p q d", d=D)

        def a_bank(tile, q):
            return ((O_ps, S_ps, up_ps[0], up_ps[1]) if prologue(tile) else (O_ps, S_ps) * 2)[q]

        def xT_bank(tile):
            return up_ps[1] if prologue(tile) else T_ps

        def s_bank(tile, k):
            return up_ps[0] if prologue(tile) and k % 2 else S_ps

        def b_bank(tile, q):
            return gate_ps[q] if prologue(tile) else O_ps

        def pT_bank(tile, k):
            return y_ps if (first(tile) and k % 2) or (prologue(tile) and k == 2 * tile - 2) else T_ps

        block = stack.enter_context(nc.Block())

        @block.sync
        def _(sp):
            sp.dma_start(probs[:, 0, :, :].rearrange("p h j -> p (h j)"), Wq).then_inc(S["wq_loaded"], 16)
            sp.dma_start(probs[0:CD, 1, :, :].rearrange("p h j -> p (h j)"), Wk).then_inc(S["wk_loaded"], 16)
            sp.dma_start(x1[:, :, :, :].rearrange("p a k d -> p (a k d)")[:, 0:8 * CD].rearrange("p (s c) -> p s c", c=CD),
                         ctx_in.rearrange("b j c -> (b j) c").rearrange("(s p) c -> p s c", p=P)
                         ).then_inc(S["ctx_loaded"], 16)
            sp.dma_start(x_raw[:, 0, :, :], x_t[0]).then_inc(S["x_loaded"], 16)
            sp.dma_start(probs[0:CD, 2, :, :].rearrange("p h j -> p (h j)"), Wv).then_inc(S["wv_loaded"], 16)
            sp.dma_start(probs[:, 3, :, :].rearrange("p h j -> p (h j)").rearrange("p (s d) -> p s d", d=D),
                         Wout.rearrange("(s p) d -> p s d", p=P)).then_inc(S["wout_loaded"], 16)
            sp.dma_start(bgu_raw[0:CH, :], bg.rearrange("e (m p) -> (e m) p", p=P)).then_inc(S["small_loaded"], 16)
            sp.dma_start(bgu_raw[CH:2 * CH, :], bu.rearrange("e (m p) -> (e m) p", p=P)).then_inc(S["small_loaded"], 16)
            sp.dma_start(bout_col[:, :], bout.rearrange("(d a) -> d a", a=1)).then_inc(S["small_loaded"], 16)
            sp.dma_start(wr_raw[:, :], Wr).then_inc(S["small_loaded"], 16)
            for n in range(3):
                sp.dma_start(bo_raw[n * E:(n + 1) * E, :], bo).then_inc(S["bo_loaded"], 16)
            sp.dma_start(wb[:, 0:4, :].rearrange("p a n -> p (a n)").rearrange("p (e m) -> p e m", e=E),
                         Wg.rearrange("e p m -> p e m")).then_inc(S["ffn_w_loaded"], 16)
            sp.dma_start(wb[:, 4:8, :].rearrange("p a n -> p (a n)").rearrange("p (e m) -> p e m", e=E),
                         Wu.rearrange("e p m -> p e m")).then_inc(S["ffn_w_loaded"], 16)
            sp.dma_start(ffn_tmp[:, 0:4, :].rearrange("p a n -> p (a n)").rearrange("p (c d) -> p c d", d=D),
                         Wo.rearrange("e (m p) d -> p (e m) d", p=P)).then_inc(S["ffn_w_loaded"], 16)
            sp.wait_ge(S["bo_lo_ready"], 1)
            sp.dma_start(as_f32(bo_hhl[0:2 * E, :]), as_f32(bo_hi[0:2 * E, :])).then_inc(S["bo_ready"], 16)
            sp.dma_start(as_f32(bo_hhl[2 * E:3 * E, :]), as_f32(bo_lo[2 * E:3 * E, :])).then_inc(S["bo_ready"], 16)
            sp.wait_ge(S["prep_ctx_lo"], 2)
            sp.dma_start(ctxT_dram[0][:, 0:NB * J], as_f32(ctxT_hi)).then_inc(S["ctxT_saved"], 16)
            sp.dma_start(ctxT_dram[1][:, 0:NB * J], as_f32(ctxT_lo)).then_inc(S["ctxT_saved"], 16)
            sp.wait_ge(S["ctxT_saved"], 32)
            sp.dma_start(x_raw[:, 1, :, :], x_t[1]).then_inc(S["x_loaded"], 16)

            def step(T, c, odd, main_on=True, early_on=True):
                y_of, main, early = T - 1, T + 1 if main_on else None, T + 2 if early_on else None

                def index(t):
                    return t if isinstance(t, int) else sp.snap(t)

                if c == 4 and live(y_of):
                    at = index(y_of)
                    sp.wait_ge(S["y_added"], y_of + 1)
                    sp.dma_start(out_t[at], y_out[:, :, :]).then_inc(S["y_stored"], 16)
                if c == 7 and live(main) and live(T + 3):
                    at = index(ahead(T + 3))
                    sp.wait_ge(S["x1_ready"], main * 2 + 2)
                    sp.dma_start(x_raw[:, 1 - odd, :, :], x_t[at]).then_inc(S["x_loaded"], 16)
                if c in (8, 10) and live(early):
                    q = (c - 8) // 2
                    sp.wait_ge(S["b_lo_done"], early * 2 + q + 1)
                    wait(sp, "ot_ready", early * 2)
                    for b in range(BT):
                        for par in range(2):
                            for src, dst in ((bs_hi, b_hi), (bs_lo, b_lo)):
                                sp.dma_start(
                                    as_f32(dst[par * J:(par + 1) * J, b, 2 * q:2 * q + 2, :]),
                                    as_f32(src[b * J:(b + 1) * J, 4 * q:4 * q + 4, :]).rearrange(
                                        "p (n r) d -> p n r d", r=2)[:, :, par, :]).then_inc(S["b_moved"], 16)
                if c == 11 and live(early) and live(T + 3) and odd:
                    at = index(ahead(T + 3) * (BT * J))
                    sp.wait_ge(S["b_ready"], early * 2 + 2)
                    cols = slice(at, at + PAIR) if isinstance(T, int) else bass.ds(at, PAIR)
                    sp.dma_start(as_f32(ctxc_hi[:, :]), ctxT_dram[0][:, cols]).then_inc(S["ctxc_loaded"], 16)
                    sp.dma_start(as_f32(ctxc_lo[:, :]), ctxT_dram[1][:, cols]).then_inc(S["ctxc_loaded"], 16)
                if c == 14 and live(main):
                    sp.wait_ge(S["wT_done"], main + 1)
                    sp.dma_start(w_dram, wT[3 * E:4 * E, :]).then_inc(S["w_saved"], 16)
                    sp.wait_ge(S["w_saved"], main * 16 + 16)
                    if isinstance(main, int) and main == 0:
                        sp.wait_ge(S["w_lo_ready"], 2)
                    for n, (e0, e1) in enumerate(WB_PARTS):
                        if e1 == E:
                            wait(sp, "gw_done", T * CH + CH)
                        sp.dma_start(wb[:, e0:e1, :], w_dram[e0:e1, :].partition_broadcast(P)
                                     ).then_inc(S[f"wb_loaded{n}"], 16)

            walk(sp, step)
            sp.wait_ge(S["y_stored"], NT * 16)
            sp.wait_ge(S["x_loaded"], (NT + 1) * 16)
            sp.wait_ge(S["ctxc_loaded"], NT // 2 * 32)

        @block.tensor
        def _(pe):
            def mm3(o, w_h, w_l, m_h, m_l, start=True, stop=True):
                nc.tensor.matmul(o, w_h, m_h, start=start, stop=False)
                nc.tensor.matmul(o, w_h, m_l, start=False, stop=False)
                return nc.tensor.matmul(o, w_l, m_h, start=False, stop=stop)

            pe.wait_ge(S["ident_ready"], 2)
            pe.wait_ge(S["wq_loaded"], 16)
            for q in range(HP):
                last = nc.tensor.transpose(gate_ps[0][:, q * P:(q + 1) * P],
                                           probs[:, 0, 2 * q:2 * q + 2, :].rearrange("p h j -> p (h j)"), ident[:, :])
            last.then_inc(S["prep_T"], 1)
            pe.wait_ge(S["wk_loaded"], 16)
            for q in range(HP):
                last = nc.tensor.transpose(gate_ps[1][:, q * CD:(q + 1) * CD],
                                           probs[0:CD, 1, 2 * q:2 * q + 2, :].rearrange("p h j -> p (h j)"),
                                           ident[0:CD, 0:CD])
            last.then_inc(S["prep_T"], 1)
            pe.wait_ge(S["ctx_loaded"], 16)
            ctx_raw = x1[:, :, :, :].rearrange("p a k d -> p (a k d)")[:, 0:8 * CD].rearrange("p (s c) -> p s c", c=CD)
            for n in range(2):
                for s in range(4):
                    last = nc.tensor.transpose((up_ps[1], y_ps)[n][0:CD, s * P:(s + 1) * P], ctx_raw[:, 4 * n + s, :],
                                               ident[:, :])
                last.then_inc(S["prep_ctx_T"], 1)
            pe.wait_ge(S["wqT_read"], 1)
            pe.wait_ge(S["wkT_read"], 1)
            wqT = y_out[:, :, :].rearrange("p k d -> p (k d)")
            for par in range(2):
                r = par * DH
                for q in range(HP):
                    last = nc.tensor.matmul((S_ps, O_ps)[par][0:CD, q * D:(q + 1) * D],
                                            ot_sb[r:r + DH, q * CD:(q + 1) * CD], wqT[r:r + DH, q * P:(q + 1) * P],
                                            start=True, stop=True)
                last.then_inc(S["prep_fold"], 1)
            pe.wait_ge(S["wv_loaded"], 16)
            for q in range(HP):
                last = nc.tensor.transpose(up_ps[0][:, q * CD:(q + 1) * CD],
                                           probs[0:CD, 2, 2 * q:2 * q + 2, :].rearrange("p h j -> p (h j)"),
                                           ident[0:CD, 0:CD])
            last.then_inc(S["prep_T"], 1)
            pe.wait_ge(S["wvT_read"], 1)
            pe.wait_ge(S["wout_loaded"], 16)
            for par in range(2):
                r = par * DH
                for q in range(HP):
                    last = nc.tensor.matmul(gate_ps[par][0:CD, q * D:(q + 1) * D],
                                            yT_sb[r:r + DH, q * CD:(q + 1) * CD],
                                            probs[r:r + DH, 3, 2 * q:2 * q + 2, :].rearrange("p h j -> p (h j)"),
                                            start=True, stop=True)
                last.then_inc(S["prep_fold"], 1)
            pe.wait_ge(S["small_loaded"], 64)
            nc.tensor.transpose(T_ps[:, 0:2 * CH], bgu_raw[:, :], ident[0:2 * CH, 0:2 * CH]).then_inc(S["bgu_T"], 1)
            pe.wait_ge(S["prep_fold_lo"], 2)
            pe.wait_ge(S["prep_ctx_lo"], 1)

            def a_piece(early, q, ps):
                for i in range(2):
                    h = 2 * q + i
                    last = mm3(ps[:, i * PAIR:(i + 1) * PAIR], m_hi[:, h, :], m_lo[:, h, :], ctxc_hi[:, :], ctxc_lo[:, :])
                last.then_inc(S["a_ready"], 1)

            def b_piece(early, odd_tile, q):
                w = slice(odd_tile * P, odd_tile * P + P)
                mm3(b_bank(early, q)[:, :], ctxc_hi[:, w], ctxc_lo[:, w],
                    n_hi[:, 4 * q:4 * q + 4, :].rearrange("p h d -> p (h d)"),
                    n_lo[:, 4 * q:4 * q + 4, :].rearrange("p h d -> p (h d)")).then_inc(S["b_ready"], 1)

            def scores(early, odd_tile, k):
                b = odd_tile * BT + k // 2
                w = slice(k * P, k * P + P)
                mm3(s_bank(early, k)[:, :], xnT_hi[:, w], xnT_lo[:, w], a_hi[:, b, :, :].rearrange("p h j -> p (h j)"),
                    a_lo[:, b, :, :].rearrange("p h j -> p (h j)")).then_inc(S["s_ready"], 1)

            def probs_T(a, k):
                pe.wait_ge(S["norm_done"], a * KT + k + 1)
                for q in range(HP):
                    last = nc.tensor.transpose(pT_bank(a, k)[:, q * P:(q + 1) * P],
                                               probs[:, k, 2 * q:2 * q + 2, :].rearrange("p h j -> p (h j)"),
                                               ident[:, :])
                last.then_inc(S["pT_ready"], 1)

            def attn_out(b):
                w = slice(b * SEQ, (b + 1) * SEQ)
                for q in range(HP):
                    last = mm3(O_ps[:, w], b_hi[:, b, q, :], b_lo[:, b, q, :], pT_hi[:, q, w], pT_lo[:, q, w],
                               start=(q == 0), stop=(q == HP - 1))
                last.then_inc(S["ot_ready"], 1)

            def step(T, c, odd, main_on=True, early_on=True):
                y_of, main, early = T - 1, T + 1 if main_on else None, T + 2 if early_on else None
                if live(T):
                    n = T * CH + c
                    rhs_h, rhs_l = xn2T_hi[:, odd, :], xn2T_lo[:, odd, :]
                    if c == 0:
                        pe.wait_ge(S["x2T_lo"], T + 1)
                    if c == 0 and isinstance(T, int) and T == 0:
                        pe.wait_ge(S["w_lo_ready"], 3)
                        pe.wait_ge(S["w_hi_ready"], 3)
                    wait(pe, "gate_done", n - 1)
                    mm3(gate_ps[c % 2][:, :], wg_hi[:, c, :], wg_lo[:, c, :], rhs_h, rhs_l).then_inc(S["gate_ready"], 1)
                    wait(pe, "h_done", n - 1)
                    mm3(up_ps[c % 2][:, :], wu_hi[:, c, :], wu_lo[:, c, :], rhs_h, rhs_l).then_inc(S["up_ready"], 1)
                t, d = (T, c - LAG) if c >= LAG else (T - 1, c - LAG + CH)
                if live(t):
                    if d == 0:
                        wait(pe, "y_read", t)
                        pe.wait_ge(S["wT_done"], t + 1)
                        if isinstance(t, int) and t == 0:
                            pe.wait_ge(S["bo_ready"], 32)
                        nc.tensor.matmul(y_ps[:, :], bo_hhl[:, :], wT_r[0:3 * E, :], start=True, stop=False)
                    pe.wait_ge(S["h_lo_done"], t * CH + d + 1)
                    mm3(y_ps[:, :], wo_hi[:, d, :], wo_lo[:, d, :], h_hi[:, d % NHB, :], h_lo[:, d % NHB, :],
                        start=False, stop=(d == CH - 1)).then_inc(S["down_done"], 1)

                if live(early):
                    if c in (5, 6) and not odd:
                        if c == 5:
                            if first(early):
                                pe.wait_ge(S["ctxc_lo_done"], 1)
                            else:
                                pe.wait_ge(S["ctxc_loaded"], early * 16)
                            wait(pe, "ot_read", early * 2)
                            wait(pe, "s_sub", early * KT)
                        elif not prologue(early):
                            pe.wait_ge(S["a_lo_done"], early * 2 + 2)
                        for q in (2 * (c - 5), 2 * (c - 5) + 1):
                            a_piece(early, q, a_bank(early, q))
                    if c == 7:
                        pe.wait_ge(S["xn_ready"], early + 1)
                        if first(early):
                            pe.wait_ge(S["a_lo_done"], 4)
                        elif not prologue(early):
                            wait(pe, "x1_ready", early * 2)
                        for k in range(KT):
                            last = nc.tensor.transpose(xT_bank(early)[:, k * P:(k + 1) * P], xn[:, k, :], ident[:, :])
                        last.then_inc(S["xT_ready"], 1)
                    if 8 <= c < 8 + KT:
                        k = c - 8
                        if k == 0:
                            pe.wait_ge(S["xT_lo"], early + 1)
                            pe.wait_ge(S["a_lo_done"], early * 2 + 4 if not odd else early * 2 + 2)
                        elif not prologue(early):
                            pe.wait_ge(S["s_sub"], early * KT + k)
                        elif k > 1:
                            pe.wait_ge(S["s_sub"], early * KT + k - 1)
                        scores(early, odd, k)
                    if c in (8, 10):
                        q = (c - 8) // 2
                        if prologue(early):
                            pe.wait_ge(S["prep_fold_lo"], 4)
                            wait(pe, "b_lo_done", early * 2)
                        elif q == 0:
                            wait(pe, "ot_read", early * 2)
                        else:
                            pe.wait_ge(S["b_lo_done"], early * 2 + 1)
                        b_piece(early, odd, q)
                if c < 2 and live(main):
                    pe.wait_ge(S["pT_lo_done"], main * KT + c + (1 if first(main) else 2))
                    probs_T(main, c + 2)
                if live(main):
                    if c == 2:
                        pe.wait_ge(S["b_moved"], main * 256 + 256)
                        pe.wait_ge(S["pT_lo_done"], main * KT + 2)
                        attn_out(0)
                    if c == 4:
                        pe.wait_ge(S["pT_lo_done"], main * KT + 4)
                        pe.wait_ge(S["ot_read"], main * 2 + 1)
                        attn_out(1)
                if c == 3 and live(y_of):
                    pe.wait_ge(S["y_read"], y_of + 1)
                    if live(main):
                        pe.wait_ge(S["pT_lo_done"], main * KT + 4)
                    for k in range(KT):
                        last = nc.tensor.transpose(T_ps[:, k * P:(k + 1) * P], yT_sb[:, k * P:(k + 1) * P], ident[:, :])
                    last.then_inc(S["yT_ready"], 1)
                if live(main):
                    if c in (4, 5):
                        b = c - 4
                        pe.wait_ge(S["ot_read"], main * 2 + b + 1)
                        if b == 0 and live(y_of):
                            pe.wait_ge(S["y_added"], y_of + 1)
                        if b == 1:
                            pe.wait_ge(S["x1_ready"], main * 2 + 1)
                        for k in (2 * b, 2 * b + 1):
                            last = nc.tensor.transpose(T_ps[:, k * P:(k + 1) * P], ot_sb[:, k * P:(k + 1) * P],
                                                       ident[:, :])
                        last.then_inc(S["ott_ready"], 1)
                    if c == 8:
                        if live(early):
                            pe.wait_ge(S["xT_lo"], early + 1)
                        pe.wait_ge(S["xn2_ready"], main + 1)
                        for k in range(KT):
                            last = nc.tensor.transpose(T_ps[:, k * P:(k + 1) * P], xn2[:, k, :], ident[:, :])
                        last.then_inc(S["x2T_ready"], 1)
                    if c == 11:
                        pe.wait_ge(S["x2T_lo"], main + 1)
                        if live(early):
                            pe.wait_ge(S["b_lo_done"], early * 2 + 2)
                        if isinstance(main, int) and main == 0:
                            pe.wait_ge(S["wr_ready"], 1)
                        for k in range(KT):
                            w = slice(k * P, k * P + P)
                            o = O_ps[:, 2 * E * k:2 * E * (k + 1)]
                            nc.tensor.matmul(o, xn2T_hi[:, 1 - odd, w], wr_hl[:, :, :].rearrange("p a e -> p (a e)"),
                                             start=True, stop=False)
                            last = nc.tensor.matmul(o[:, 0:E], xn2T_lo[:, 1 - odd, w], wr_hl[:, 0, :],
                                                    start=False, stop=True)
                        last.then_inc(S["router_ready"], 1)
                    if c == 13:
                        pe.wait_ge(S["w_ready"], main + 1)
                        for k in range(KT):
                            last = nc.tensor.transpose(T_ps[0:4 * E, k * P:(k + 1) * P], wst[:, k, :], ident[:, :])
                        last.then_inc(S["wT_ready"], 1)
                if c >= 14 and live(early):
                    if c == 14 and live(main):
                        pe.wait_ge(S["wT_done"], main + 1)
                    if c == 14 and first(early):
                        pe.wait_ge(S["bgu_ready"], 1)
                        pe.wait_ge(S["prep_ctx_lo"], 2)
                    if c == 15 and prologue(early) and not first(early):
                        pe.wait_ge(S["wT_done"], 1)
                    elif c == 15 and not first(early):
                        pe.wait_ge(S["pT_lo_done"], early * KT + 1)
                    probs_T(early, c - 14)

            walk(pe, step)

        @block.scalar
        def _(act):
            copy = nc.scalar.copy
            act.wait_ge(S["prep_T"], 1)
            copy(y_out[:, :, :].rearrange("p k d -> p (k d)"), gate_ps[0][:, :]).then_inc(S["wqT_read"], 1)
            act.wait_ge(S["prep_ctx_T"], 1)
            copy(ctxc_hi[:, :], up_ps[1][0:CD, 0:PAIR])
            copy(ctxT_hi[:, 0:512], up_ps[1][0:CD, :]).then_inc(S["prep_ctx_hi"], 1)

            def fold_hi(n):
                act.wait_ge(S["prep_fold"], n + 1)
                dst = (m_hi, m_hi, n_hi, n_hi)[n][:, :, :].rearrange("p (q r) d -> p r q d", r=2)[:, n % 2, :, :]
                nc.scalar.mul(dst, folded(n), SCALE if n < 2 else 1.0).then_inc(S["prep_fold_hi"], 1)

            fold_hi(0)
            fold_hi(1)
            act.wait_ge(S["prep_T"], 3)
            copy(yT_sb[:, 0:HP * CD], up_ps[0][:, 0:HP * CD]).then_inc(S["wvT_read"], 1)
            copy(ctxT_hi[:, 512:1024], y_ps[0:CD, :]).then_inc(S["prep_ctx_hi"], 1)

            def xn_apply(early, odd):
                act.wait_ge(S["ln1_rstd"], early + 1)
                act.wait_ge(S["x_loaded"], early * 16 + 16)
                for k in range(KT):
                    last = nc.scalar.activation(xn[:, k, :], x_raw[:, odd, k, :], ACT.Identity,
                                                bias=nmr[:, k:k + 1], scale=rstd[:, k:k + 1])
                last.then_inc(S["xn_ready"], 1)

            xn_apply(0, 0)
            fold_hi(2)
            fold_hi(3)
            act.wait_ge(S["bgu_T"], 1)
            copy(bgu[:, :, :].rearrange("p a c -> p (a c)"), T_ps[:, 0:2 * CH]).then_inc(S["bgu_ready"], 1)
            act.wait_ge(S["small_loaded"], 64)
            copy(wr_hl[:, 0, :], wr_raw[:, :]).then_inc(S["wr_hi_ready"], 1)
            act.wait_ge(S["bo_loaded"], 48)
            copy(bo_hi[:, :], bo_raw[:, :]).then_inc(S["bo_hi_ready"], 1)

            def step(T, c, odd, main_on=True, early_on=True):
                y_of, main, early = T - 1, T + 1 if main_on else None, T + 2 if early_on else None
                if c == 3 and live(y_of):
                    act.wait_ge(S["down_done"], y_of * CH + CH)
                    copy(yT_sb[:, :], y_ps[:, :]).then_inc(S["y_read"], 1)
                if live(T):
                    n = T * CH + c
                    act.wait_ge(S["gate_ready"], n + 1)
                    wait(act, "gw_done", n - 1)
                    nc.scalar.activation(gate_sb(c), gate_ps[c % 2][:, :], ACT.Silu, bias=bgu[:, 0, c:c + 1]
                                         ).then_inc(S["gate_done"], 1)
                t, d = (T, c - 1) if c >= 1 else (T - 1, CH - 1)
                if live(t):
                    act.wait_ge(S["h_done"], t * CH + d + 1)
                    wait(act, "down_done", t * CH + d - NHB + 1)
                    copy(h_hi[:, d % NHB, :], h_sb(d)).then_inc(S["h_hi_done"], 1)
                if first(early) and 9 <= c < 12:
                    if c == 9:
                        act.wait_ge(S["ffn_w_loaded"], 48)
                    w, src = ((wg_hi, wb[:, 0:4, :]), (wu_hi, wb[:, 4:8, :]), (wo_hi, ffn_tmp[:, 0:4, :]))[c - 9]
                    copy(w[:, :, :].rearrange("p c n -> p (c n)"), src.rearrange("p a n -> p (a n)")
                         ).then_inc(S["w_hi_ready"], 1)
                if live(main) and c == 7:
                    act.wait_ge(S["ln2_rstd"], main + 1)
                    for k in range(KT):
                        last = nc.scalar.activation(xn2[:, k, :], x1[:, 1 - odd, k, :], ACT.Identity,
                                                    bias=nmr[:, KT + k:KT + k + 1], scale=rstd[:, KT + k:KT + k + 1])
                    last.then_inc(S["xn2_ready"], 1)
                if live(early):
                    if c == 6 and not first(early):
                        xn_apply(early, odd)
                    if c in (5, 6) and not odd:
                        for i in range(2):
                            q = 2 * (c - 5) + i
                            act.wait_ge(S["a_ready"], early * 2 + q + 1)
                            copy(a_hi[:, :, 2 * q:2 * q + 2, :].rearrange("p b h j -> p h b j"),
                                 a_bank(early, q)[:, :].rearrange("p (h b j) -> p h b j", h=2, j=J)
                                 ).then_inc(S["a_hi_done"], 1)
                    if c == 7:
                        act.wait_ge(S["xT_ready"], early + 1)
                        copy(xnT_hi[:, :], xT_bank(early)[:, :]).then_inc(S["xT_hi"], 1)
                    if c in (8, 10):
                        q = (c - 8) // 2
                        act.wait_ge(S["b_ready"], early * 2 + q + 1)
                        wait(act, "b_moved", early * 256)
                        copy(bs_hi[:, 4 * q:4 * q + 4, :].rearrange("p h d -> p (h d)"), b_bank(early, q)[:, :]
                             ).then_inc(S["b_hi_done"], 1)
                if live(main):
                    if c == 12:
                        act.wait_ge(S["logits_ready"], main + 1)
                        nc.scalar.activation(lg_e[:, :, :], lg_d[:, :, :], ACT.Exp).then_inc(S["route_exp"], 1)
                if live(early):
                    if c == 12:
                        for i in range(2):
                            act.wait_ge(S["s_sub"], early * KT + 2 * i + 2)
                            last = nc.scalar.activation(probs[:, 2 * i:2 * i + 2, :, :], probs[:, 2 * i:2 * i + 2, :, :],
                                                        ACT.Exp)
                            last.then_inc(S["exp_done"], 1)
                for a, k, on in ((early, c - 14, c >= 14), (main, c + 2, c < 2)):
                    if on and live(a):
                        act.wait_ge(S["pT_ready"], a * KT + k + 1)
                        copy(pT_hi[:, :, k * P:(k + 1) * P], pT_bank(a, k)[:, :].rearrange("p (q n) -> p q n", q=HP)
                             ).then_inc(S["pT_hi_done"], 1)
                if live(main):
                    if c in (2, 4):
                        b = (c - 2) // 2
                        act.wait_ge(S["ot_ready"], main * 2 + b + 1)
                        nc.scalar.activation(ot_sb[:, b * SEQ:(b + 1) * SEQ], O_ps[:, b * SEQ:(b + 1) * SEQ], ACT.Identity,
                                             bias=bout_col[:, 0:1]).then_inc(S["ot_read"], 1)
                    if c == 8:
                        act.wait_ge(S["x2T_ready"], main + 1)
                        copy(xn2T_hi[:, 1 - odd, :], T_ps[:, :]).then_inc(S["x2T_hi"], 1)

            walk(act, step)

        @block.gpsimd
        def _(pool):
            nc.gpsimd.memset(ident[:, :], 0.0).then_inc(S["ident_ready"], 1)
            pool.wait_ge(S["ident_ready"], 1)
            nc.gpsimd.affine_select(out=ident[:, :], in_=ident[:, :], compare_op=ALU.not_equal, fill=1.0, base=0,
                                    pattern=[[-1, P]], channel_multiplier=1).then_inc(S["ident_ready"], 1)
            nc.gpsimd.memset(m_half[:, :], -0.5).then_inc(S["half_ready"], 1)
            nc.gpsimd.iota(iota_e[:, :, :], [[0, KT], [1, E]], base=0, channel_multiplier=0,
                           allow_small_or_imprecise_dtypes=True).then_inc(S["iota_ready"], 1)
            pool.wait_ge(S["small_loaded"], 64)
            pool.wait_ge(S["half_ready"], 1)

            def w_lo(n):
                hi, lo, src = ((wg_hi, wg_lo, wb[:, 0:4, :]), (wu_hi, wu_lo, wb[:, 4:8, :]),
                               (wo_hi, wo_lo, ffn_tmp[:, 0:4, :]))[n]
                pool.wait_ge(S["w_hi_ready"], n + 1)
                nc.gpsimd.tensor_tensor(lo[:, :, :].rearrange("p c n -> p (c n)"), src.rearrange("p a n -> p (a n)"),
                                        as_f32(hi[:, :, :].rearrange("p c n -> p (c n)")), ALU.subtract
                                        ).then_inc(S["w_lo_ready"], 1)

            def step(T, c, odd, main_on=True, early_on=True):
                main, early = T + 1 if main_on else None, T + 2 if early_on else None
                if live(T):
                    n = T * CH + c
                    for part, (e0, _) in enumerate(WB_PARTS):
                        if c == e0 * MC:
                            pool.wait_ge(S[f"wb_loaded{part}"], T * 16 + 16)
                    pool.wait_ge(S["gate_done"], n + 1)
                    wait(pool, "h_done", n - 1)
                    nc.gpsimd.tensor_tensor(gw_sb(c), gate_sb(c), wb[:, c // MC, :], ALU.mult).then_inc(S["gw_done"], 1)
                if live(early):
                    if c == 5:
                        pool.wait_ge(S["ln1_stats"], early * 4 + 4)
                        nc.gpsimd.tensor_tensor(rstd[:, 0:KT], var_eps[:, 0:KT], m_half[:, 0:KT], ALU.pow
                                                ).then_inc(S["ln1_pow"], 1)
                        pool.wait_ge(S["ln1_pow"], early + 1)
                        nc.gpsimd.tensor_tensor(nmr[:, 0:KT], neg_mean[:, 0:KT], rstd[:, 0:KT], ALU.mult
                                                ).then_inc(S["ln1_rstd"], 1)
                    if first(early) and c == 9:
                        w_lo(0)
                    if c in (13, 14, 15):
                        norm(early, c - 13)
                if live(main):
                    if c == 0:
                        norm(main, 3)
                    if first(main) and c in (1, 2):
                        w_lo(c)
                    if c == 6:
                        w = slice(KT, 2 * KT)
                        pool.wait_ge(S["ln2_stats"], main * 4 + 4)
                        nc.gpsimd.tensor_tensor(rstd[:, w], var_eps[:, w], m_half[:, w], ALU.pow
                                                ).then_inc(S["ln2_pow"], 1)
                        pool.wait_ge(S["ln2_pow"], main + 1)
                        nc.gpsimd.tensor_tensor(nmr[:, w], neg_mean[:, w], rstd[:, w], ALU.mult
                                                ).then_inc(S["ln2_rstd"], 1)

            def norm(a, k):
                pool.wait_ge(S["inv_done"], a * 2 + k // 2 + 1)
                nc.gpsimd.tensor_tensor(probs[:, k, :, :], probs[:, k, :, :],
                                        r_inv[:, k, :].unsqueeze(2).to_broadcast([P, H, J]), ALU.mult
                                        ).then_inc(S["norm_done"], 1)

            walk(pool, step)

        @block.vector
        def _(dve):
            V = nc.vector

            def stats(src, col, ks, base, name):
                for k in ks:
                    last = V.bn_stats(bn[:, col + k, :], src(k))
                last.then_inc(S[name], 1)
                w = slice(col + ks[0], col + ks[-1] + 1)
                dve.wait_ge(S[name], base + 1)
                V.tensor_tensor(m_diff[:, w], bn[:, w, 1], bn[:, w, 4], ALU.subtract)
                V.tensor_tensor(v_sum[:, w], bn[:, w, 2], bn[:, w, 5], ALU.add).then_inc(S[name], 1)
                dve.wait_ge(S[name], base + 2)
                V.scalar_tensor_tensor(m_sq[:, w], m_diff[:, w], 0.25, m_diff[:, w], ALU.mult, ALU.mult)
                V.tensor_scalar(v_eps[:, w], v_sum[:, w], 1.0 / D, EPS, ALU.mult, ALU.add)
                V.scalar_tensor_tensor(neg_mean[:, w], m_diff[:, w], -0.5, bn[:, w, 4], ALU.mult, ALU.subtract
                                       ).then_inc(S[name], 1)
                dve.wait_ge(S[name], base + 3)
                V.tensor_tensor(var_eps[:, w], v_eps[:, w], m_sq[:, w], ALU.add).then_inc(S[name], 1)

            def ctx_lo(n):
                dve.wait_ge(S["prep_ctx_hi"], n + 1)
                w = slice(n * 512, (n + 1) * 512)
                V.tensor_tensor(ctxT_lo[:, w], (up_ps[1], y_ps)[n][0:CD, :], as_f32(ctxT_hi[:, w]), ALU.subtract
                                ).then_inc(S["prep_ctx_lo"], 1)

            def fold_lo(n):
                dve.wait_ge(S["prep_fold_hi"], n + 1)
                hi, lo = ((m_hi, m_lo), (m_hi, m_lo), (n_hi, n_lo), (n_hi, n_lo))[n]
                hi, lo = (w[:, :, :].rearrange("p (q r) d -> p r q d", r=2)[:, n % 2, :, :] for w in (hi, lo))
                V.scalar_tensor_tensor(lo, folded(n), SCALE if n < 2 else 1.0, as_f32(hi), ALU.mult, ALU.subtract
                                       ).then_inc(S["prep_fold_lo"], 1)

            def ln1_stats(early, odd):
                dve.wait_ge(S["x_loaded"], early * 16 + 16)
                wait(dve, "ln1_rstd", early)
                stats(lambda k: x_raw[:, odd, k, :], 0, range(KT), early * 4, "ln1_stats")

            dve.wait_ge(S["prep_T"], 2)
            V.tensor_copy(ot_sb[:, 0:HP * CD], gate_ps[1][:, 0:HP * CD]).then_inc(S["wkT_read"], 1)
            dve.wait_ge(S["prep_ctx_hi"], 1)
            V.tensor_tensor(ctxc_lo[:, :], up_ps[1][0:CD, 0:PAIR], as_f32(ctxc_hi[:, :]), ALU.subtract
                            ).then_inc(S["ctxc_lo_done"], 1)
            ctx_lo(0)
            ln1_stats(0, 0)
            fold_lo(0)
            fold_lo(1)
            fold_lo(2)
            fold_lo(3)
            ctx_lo(1)
            dve.wait_ge(S["wr_hi_ready"], 1)
            V.tensor_tensor(wr_hl[:, 1, :], wr_raw[:, :], as_f32(wr_hl[:, 0, :]), ALU.subtract).then_inc(S["wr_ready"], 1)
            dve.wait_ge(S["bo_hi_ready"], 1)
            V.tensor_tensor(bo_lo[:, :], bo_raw[:, :], as_f32(bo_hi[:, :]), ALU.subtract).then_inc(S["bo_lo_ready"], 1)
            dve.wait_ge(S["iota_ready"], 1)
            dve.wait_ge(S["bgu_ready"], 1)

            def split_lo(lo, full, hi):
                return V.tensor_tensor(lo, full, as_f32(hi), ALU.subtract)

            ROUTE = 8

            def step(T, c, odd, main_on=True, early_on=True):
                y_of, main, early = T - 1, T + 1 if main_on else None, T + 2 if early_on else None

                for a, k, on in ((early, 0, c == 15), (main, c + 1, c < 3)):
                    if on and live(a):
                        dve.wait_ge(S["pT_hi_done"], a * KT + k + 1)
                        split_lo(pT_lo[:, :, k * P:(k + 1) * P], pT_bank(a, k)[:, :].rearrange("p (q n) -> p q n", q=HP),
                                 pT_hi[:, :, k * P:(k + 1) * P]).then_inc(S["pT_lo_done"], 1)
                if c == 4 and live(y_of):
                    dve.wait_ge(S["yT_ready"], y_of + 1)
                    V.tensor_tensor(y_out[:, :, :].rearrange("p k d -> p (k d)"), T_ps[:, :],
                                    x1[:, 1 - odd, :, :].rearrange("p k d -> p (k d)"), ALU.add).then_inc(S["y_added"], 1)
                if live(main):
                    if c in (5, 6):
                        b = c - 5
                        dve.wait_ge(S["ott_ready"], main * 2 + b + 1)
                        dve.wait_ge(S["x_loaded"], main * 16 + 16)
                        V.tensor_tensor(x1[:, 1 - odd, 2 * b:2 * b + 2, :],
                                        T_ps[:, b * SEQ:(b + 1) * SEQ].rearrange("p (k d) -> p k d", d=D),
                                        x_raw[:, 1 - odd, 2 * b:2 * b + 2, :], ALU.add).then_inc(S["x1_ready"], 1)
                if live(early):
                    if c == 8:
                        dve.wait_ge(S["xT_hi"], early + 1)
                        split_lo(xnT_lo[:, :], xT_bank(early)[:, :], xnT_hi[:, :]).then_inc(S["xT_lo"], 1)
                    if c in (6, 7) and not odd:
                        for i in range(2):
                            q = 2 * (c - 6) + i
                            dve.wait_ge(S["a_hi_done"], early * 2 + q + 1)
                            w = (slice(None), slice(None), slice(2 * q, 2 * q + 2), slice(None))
                            split_lo(a_lo[w].rearrange("p b h j -> p h b j"),
                                     a_bank(early, q)[:, :].rearrange("p (h b j) -> p h b j", h=2, j=J),
                                     a_hi[w].rearrange("p b h j -> p h b j")).then_inc(S["a_lo_done"], 1)
                    if 9 <= c < 9 + KT:
                        k = c - 9
                        s3 = s_bank(early, k)[:, :].rearrange("p (h j) -> p h j", h=H)
                        dve.wait_ge(S["s_ready"], early * KT + k + 1)
                        V.tensor_reduce(s_max[:, k, :], s3, AX_X, ALU.max).then_inc(S["s_maxed"], 1)
                        dve.wait_ge(S["s_maxed"], early * KT + k + 1)
                        V.tensor_tensor(probs[:, k, :, :], s3, s_max[:, k, :].unsqueeze(2).to_broadcast([P, H, J]),
                                        ALU.subtract).then_inc(S["s_sub"], 1)
                if live(main) and c == 9:
                    dve.wait_ge(S["x2T_hi"], main + 1)
                    split_lo(xn2T_lo[:, 1 - odd, :], T_ps[:, :], xn2T_hi[:, 1 - odd, :]).then_inc(S["x2T_lo"], 1)
                if live(early) and c in (9, 11):
                    q = (c - 9) // 2
                    dve.wait_ge(S["b_hi_done"], early * 2 + q + 1)
                    w = slice(4 * q, 4 * q + 4)
                    split_lo(bs_lo[:, w, :].rearrange("p h d -> p (h d)"), b_bank(early, q)[:, :],
                             bs_hi[:, w, :].rearrange("p h d -> p (h d)")).then_inc(S["b_lo_done"], 1)
                if live(main) and c == 12:
                    at = main * ROUTE
                    o = O_ps[:, 0:KT * 2 * E].rearrange("p (k a e) -> p k a e", k=KT, a=2)
                    dve.wait_ge(S["router_ready"], main + 1)
                    V.tensor_copy(lg_lo[:, :, :], o[:, :, 1, :]).then_inc(S["route_step"], 1)
                    dve.wait_ge(S["route_step"], at + 1)
                    V.tensor_tensor(lg[:, :, :], o[:, :, 0, :], lg_lo[:, :, :], ALU.add).then_inc(S["route_step"], 1)
                    dve.wait_ge(S["route_step"], at + 2)
                    V.tensor_copy(lg_lo[:, :, :], lg[:, :, :])
                    for k in range(KT):
                        last = V.max(top[:, k, :], lg[:, k, :])
                    last.then_inc(S["route_step"], 1)
                    dve.wait_ge(S["route_step"], at + 3)
                    V.tensor_tensor(lg_d[:, :, :], lg[:, :, :], top[:, :, 0:1].to_broadcast([P, KT, E]), ALU.subtract
                                    ).then_inc(S["logits_ready"], 1)
                if live(main) and c == 13:
                    at = main * ROUTE
                    dve.wait_ge(S["route_exp"], main + 1)
                    dve.wait_ge(S["route_step"], at + 6)
                    V.tensor_tensor(sel_e[:, :, :], sel[:, :, :], lg_e[:, :, :], ALU.mult)
                    V.tensor_reduce(den_a[:, :], lg_e[:, :, :], AX_X, ALU.add).then_inc(S["route_step"], 1)
                    dve.wait_ge(S["route_step"], at + 7)
                    V.tensor_reduce(den_b[:, :], sel_e[:, :, :], AX_X, ALU.add).then_inc(S["route_step"], 1)
                    dve.wait_ge(S["route_step"], at + 8)
                    V.scalar_tensor_tensor(den[:, :], den_a[:, :], NORM_EPS, den_b[:, :], ALU.mult, ALU.add
                                           ).then_inc(S["w_steps"], 1)
                    dve.wait_ge(S["w_steps"], main * 3 + 1)
                    V.reciprocal(den_inv[:, :], den[:, :]).then_inc(S["w_steps"], 1)
                    dve.wait_ge(S["w_steps"], main * 3 + 2)
                    V.tensor_tensor(wst[:, :, 3 * E:4 * E], sel_e[:, :, :],
                                    den_inv[:, :].unsqueeze(2).to_broadcast([P, KT, E]), ALU.mult)
                    V.tensor_tensor(wst[:, :, 0:E].bitcast(F32R), sel_e[:, :, :],
                                    den_inv[:, :].unsqueeze(2).to_broadcast([P, KT, E]), ALU.mult)
                    V.tensor_tensor(wst[:, :, 2 * E:3 * E].bitcast(F32R), sel_e[:, :, :],
                                    den_inv[:, :].unsqueeze(2).to_broadcast([P, KT, E]), ALU.mult
                                    ).then_inc(S["w_steps"], 1)
                    dve.wait_ge(S["w_steps"], main * 3 + 3)
                    V.tensor_tensor(wst[:, :, E:2 * E], wst[:, :, 3 * E:4 * E], wst[:, :, 0:E], ALU.subtract
                                    ).then_inc(S["w_ready"], 1)
                if live(y_of) and c == 14:
                    dve.wait_ge(S["y_stored"], y_of * 16 + 16)
                if live(main) and c == 14:
                    dve.wait_ge(S["wT_ready"], main + 1)
                    wait(dve, "w_saved", main * 16)
                    V.tensor_copy(wT[:, :], T_ps[0:4 * E, :])
                    V.tensor_copy(wT_r[:, :], T_ps[0:4 * E, :]).then_inc(S["wT_done"], 1)
                t, d = (T, c - 1) if c >= 1 else (T - 1, c - 1 + CH)
                if live(t):
                    dve.wait_ge(S["gw_done"], t * CH + d + 1)
                    dve.wait_ge(S["up_ready"], t * CH + d + 1)
                    wait(dve, "h_lo_done", t * CH + d - 1)
                    V.scalar_tensor_tensor(h_sb(d), up_ps[d % 2][:, :], bgu[:, 1, d:d + 1], gw_sb(d), ALU.add, ALU.mult
                                           ).then_inc(S["h_done"], 1)
                t, d = (T, c - 2) if c >= 2 else (T - 1, c - 2 + CH)
                if live(t):
                    dve.wait_ge(S["h_hi_done"], t * CH + d + 1)
                    split_lo(h_lo[:, d % NHB, :], h_sb(d), h_hi[:, d % NHB, :]).then_inc(S["h_lo_done"], 1)
                if live(early) and c == 5 and not first(early):
                    ln1_stats(early, odd)
                if live(main) and c == 6:
                    dve.wait_ge(S["x1_ready"], main * 2 + 2)
                    stats(lambda k: x1[:, 1 - odd, k, :], KT, range(KT), main * 4, "ln2_stats")
                if live(main) and c == 12:
                    at = main * ROUTE
                    for k in range(KT):
                        last = V.max_index(top_at[:, k, :], top[:, k, :], lg[:, k, :])
                    last.then_inc(S["route_step"], 1)
                    dve.wait_ge(S["route_step"], at + 4)
                    V.tensor_tensor(oh1[:, :, :], iota_e[:, :, :], top_at[:, :, 0:1].to_broadcast([P, KT, E]),
                                    ALU.is_equal)
                    V.tensor_tensor(oh2[:, :, :], iota_e[:, :, :], top_at[:, :, 1:2].to_broadcast([P, KT, E]),
                                    ALU.is_equal).then_inc(S["route_step"], 1)
                    dve.wait_ge(S["route_step"], at + 5)
                    V.tensor_tensor(sel[:, :, :], oh1[:, :, :], oh2[:, :, :], ALU.add).then_inc(S["route_step"], 1)
                if live(early) and c in (13, 14):
                    i = c - 13
                    w = slice(2 * i, 2 * i + 2)
                    dve.wait_ge(S["exp_done"], early * 2 + i + 1)
                    V.tensor_reduce(r_sum[:, w, :], probs[:, w, :, :], AX_X, ALU.add).then_inc(S["sums_done"], 1)
                    dve.wait_ge(S["sums_done"], early * 2 + i + 1)
                    V.reciprocal(r_inv[:, w, :], r_sum[:, w, :]).then_inc(S["inv_done"], 1)

            walk(dve, step)


_INS = ['x', 'ctx_768', 'L0_xattn_Wq', 'L0_xattn_Wk', 'L0_xattn_Wv', 'L0_xattn_Wout', 'L0_xattn_bout',
        'L0_ffn_W_router', 'L0_ffn_W_gate', 'L0_ffn_b_gate', 'L0_ffn_W_up', 'L0_ffn_b_up', 'L0_ffn_W_out',
        'L0_ffn_b_out']
_OUTS = [((16, 256, 128), 'float32')]


def kernel(**inputs):
    import numpy as _np
    import concourse.bacc as _bacc
    from concourse import mybir as _mybir
    from concourse.bass_utils import run_bass_kernel_spmd as _run

    nc = _bacc.Bacc("TRN2", target_bir_lowering=False, num_devices=1)
    arrays, args = {}, []
    for name in _INS:
        a = _np.ascontiguousarray(inputs[name])
        arrays[f"in_{name}_dram"] = a
        args.append(nc.dram_tensor(f"in_{name}_dram", a.shape, _mybir.dt.from_np(a.dtype), kind="ExternalInput").ap())
    for i, (shape, dtype) in enumerate(_OUTS):
        dt = _mybir.dt.from_np(_np.dtype(dtype))
        args.append(nc.dram_tensor(f"out_{i}_dram", shape, dt, kind="ExternalOutput").ap())
    xattn_moe_kernel(nc, *args)
    r = _run(nc, [arrays], core_ids=[0])
    got = tuple(r.results[0][f"out_{i}_dram"] for i in range(len(_OUTS)))
    return got[0]
```

```python
from contextlib import ExitStack

import concourse.bass as bass
from concourse import mybir

F32 = mybir.dt.float32
F32R = mybir.dt.float32r
U32 = mybir.dt.uint32
ALU = mybir.AluOpType
ACT = mybir.ActivationFunctionType
AX_X = mybir.AxisListType.X

P = 128
EPS = 1e-5
NORM_EPS = 1e-8


def xattn_moe_kernel(nc, x, ctx_in, Wq, Wk, Wv, Wout, bout, Wr, Wg, bg, Wu, bu, Wo, bo, out):
    NB, SEQ, D = x.shape
    _, J, CD = ctx_in.shape
    INNER = Wq.shape[1]
    DH = 64
    H = INNER // DH
    HP = H // 2
    E, _, M = Wg.shape
    MC = M // P
    TOK = 512
    KT = TOK // P
    BT = TOK // SEQ
    NT = NB * SEQ // TOK
    CH = E * MC
    HB = H // 2
    SCALE = DH ** -0.5
    LAG = 3
    WB_PARTS = ((0, 1), (1, 4), (4, 8))
    NHB = 4
    PAIR = 2 * BT * J
    assert D == P and CH == 16 and J * 2 == P and TOK == 512 and NT % 2 == 0 and E == 8 and BT == 2

    x_t = x.rearrange("(t b) (s p) d -> t p (b s) d", b=BT, p=P)
    out_t = out.rearrange("(t b) (s p) d -> t p (b s) d", b=BT, p=P)
    ctxT_dram = [nc.dram_tensor(f"ctxT_{n}_scratch", (CD, (NT + 1) * BT * J), F32, kind="Internal").ap()
                 for n in ("hi", "lo")]
    w_dram = nc.dram_tensor("expert_weights_scratch", (E, TOK), F32, kind="Internal").ap()

    with ExitStack() as stack:
        def sb(name, shape, dt=F32):
            return stack.enter_context(nc.sbuf_tensor(name, shape, dt))

        def sem(name):
            return stack.enter_context(nc.semaphore(name))

        ident = sb("ident", [P, P])
        wg_hi = sb("wg_hi", [P, CH, P], F32R)
        wg_lo = sb("wg_lo", [P, CH, P], F32R)
        wu_hi = sb("wu_hi", [P, CH, P], F32R)
        wu_lo = sb("wu_lo", [P, CH, P], F32R)
        wo_hi = sb("wo_hi", [P, CH, D], F32R)
        wo_lo = sb("wo_lo", [P, CH, D], F32R)
        m_hi = sb("m_hi", [CD, H, D], F32R)
        m_lo = sb("m_lo", [CD, H, D], F32R)
        n_hi = sb("n_hi", [CD, H, D], F32R)
        n_lo = sb("n_lo", [CD, H, D], F32R)
        wr_raw = sb("wr_raw", [P, E])
        wr_hl = sb("wr_hl", [P, 2, E], F32R)
        bout_col = sb("bout_col", [D, 1])
        bgu_raw = sb("bgu_raw", [2 * CH, P])
        bgu = sb("bgu", [P, 2, CH])
        bo_raw = sb("bo_raw", [3 * E, D])
        bo_hi = sb("bo_hi", [3 * E, D], F32R)
        bo_lo = sb("bo_lo", [3 * E, D], F32R)
        bo_hhl = sb("bo_hhl", [3 * E, D], F32R)
        iota_e = sb("iota_e", [P, KT, E])

        x_raw = sb("x_raw", [P, 2, KT, D])
        bn = sb("bn", [P, 2 * KT, 6])
        m_diff = sb("m_diff", [P, 2 * KT])
        m_sq = sb("m_sq", [P, 2 * KT])
        v_sum = sb("v_sum", [P, 2 * KT])
        v_eps = sb("v_eps", [P, 2 * KT])
        var_eps = sb("var_eps", [P, 2 * KT])
        neg_mean = sb("neg_mean", [P, 2 * KT])
        rstd = sb("rstd", [P, 2 * KT])
        nmr = sb("nmr", [P, 2 * KT])
        m_half = sb("m_half", [P, 2 * KT])
        xn = sb("xn", [P, KT, D])
        xnT_hi = sb("xnT_hi", [P, TOK], F32R)
        xnT_lo = sb("xnT_lo", [P, TOK], F32R)
        ctxc_hi = sb("ctxc_hi", [CD, PAIR], F32R)
        ctxc_lo = sb("ctxc_lo", [CD, PAIR], F32R)
        a_hi = sb("a_hi", [P, 2 * BT, H, J], F32R)
        a_lo = sb("a_lo", [P, 2 * BT, H, J], F32R)
        bs_hi = sb("bs_hi", [P, H, D], F32R)
        bs_lo = sb("bs_lo", [P, H, D], F32R)
        b_hi = sb("b_hi", [P, BT, HP, D], F32R)
        b_lo = sb("b_lo", [P, BT, HP, D], F32R)
        s_max = sb("s_max", [P, KT, H])
        probs = sb("probs", [P, KT, H, J])
        r_sum = sb("r_sum", [P, KT, H])
        r_inv = sb("r_inv", [P, KT, H])
        pT_hi = sb("pT_hi", [P, HP, TOK], F32R)
        pT_lo = sb("pT_lo", [P, HP, TOK], F32R)
        ctxT_hi = pT_hi[0:CD, :, :].rearrange("p q n -> p (q n)")[:, 0:NB * J]
        ctxT_lo = pT_lo[0:CD, :, :].rearrange("p q n -> p (q n)")[:, 0:NB * J]
        ot_sb = sb("ot_sb", [P, TOK])
        x1 = sb("x1", [P, 2, KT, D])
        xn2 = sb("xn2", [P, KT, D])
        xn2T_hi = sb("xn2T_hi", [P, 2, TOK], F32R)
        xn2T_lo = sb("xn2T_lo", [P, 2, TOK], F32R)

        lg_lo = sb("lg_lo", [P, KT, E])
        lg = sb("lg", [P, KT, E])
        top = sb("top", [P, KT, 8])
        top_at = sb("top_at", [P, KT, 8], U32)
        lg_d = sb("lg_d", [P, KT, E])
        lg_e = sb("lg_e", [P, KT, E])
        oh1 = sb("oh1", [P, KT, E])
        oh2 = sb("oh2", [P, KT, E])
        sel = sb("sel", [P, KT, E])
        sel_e = sb("sel_e", [P, KT, E])
        den_a = sb("den_a", [P, KT])
        den_b = sb("den_b", [P, KT])
        den = sb("den", [P, KT])
        den_inv = sb("den_inv", [P, KT])
        wst = sb("wst", [P, KT, 4 * E])
        wT = sb("wT", [4 * E, TOK])
        wT_r = sb("wT_r", [4 * E, TOK], F32R)
        wb = sb("wb", [P, E, TOK])

        ffn_tmp = sb("ffn_tmp", [P, 6, TOK])
        h_hi = sb("h_hi", [P, NHB, TOK], F32R)
        h_lo = sb("h_lo", [P, NHB, TOK], F32R)
        yT_sb = sb("yT_sb", [P, TOK])
        y_out = sb("y_out", [P, KT, D])

        def gate_sb(c):
            return ffn_tmp[:, c % 2, :]

        def gw_sb(c):
            return ffn_tmp[:, 2 + c % 2, :]

        def h_sb(c):
            return ffn_tmp[:, 4 + c % 2, :]

        def bank(name):
            return stack.enter_context(nc.psum_tensor(name, [P, 512], F32))

        gate_ps = [bank("gate_ps0"), bank("gate_ps1")]
        up_ps = [bank("up_ps0"), bank("up_ps1")]
        y_ps = bank("y_ps")
        T_ps = bank("T_ps")
        S_ps = bank("S_ps")
        O_ps = bank("O_ps")

        names = (
            "x_loaded wq_loaded wk_loaded wv_loaded wout_loaded ctx_loaded small_loaded ffn_w_loaded bo_loaded "
            "ident_ready prep_T wqT_read wkT_read wvT_read "
            "prep_ctx_T prep_ctx_hi prep_ctx_lo ctxc_lo_done prep_fold prep_fold_hi prep_fold_lo ctxT_saved ctxc_loaded "
            "bgu_T bgu_ready "
            "w_hi_ready w_lo_ready wr_hi_ready wr_ready bo_hi_ready bo_lo_ready bo_ready iota_ready half_ready "
            "ln1_stats ln1_pow ln1_rstd xn_ready xT_ready xT_hi xT_lo "
            "a_ready a_hi_done a_lo_done b_ready b_hi_done b_lo_done b_moved "
            "s_ready s_maxed s_sub exp_done sums_done inv_done norm_done pT_ready pT_hi_done pT_lo_done "
            "ot_ready ot_read ott_ready x1_ready ln2_stats ln2_pow ln2_rstd xn2_ready "
            "x2T_ready x2T_hi x2T_lo router_ready route_step w_steps logits_ready route_exp w_ready wT_ready wT_done "
            "w_saved wb_loaded0 wb_loaded1 wb_loaded2 "
            "gate_ready gate_done gw_done up_ready h_done h_hi_done h_lo_done down_done "
            "y_read yT_ready y_added y_stored"
        ).split()
        S = {n: sem(n) for n in names}

        def wait(eng, name, value):
            if not isinstance(value, int) or value > 0:
                eng.wait_ge(S[name], value)

        def live(t):
            return t is not None and (not isinstance(t, int) or 0 <= t < NT)

        def first(t):
            return isinstance(t, int) and t == 0

        def prologue(t):
            return isinstance(t, int) and t < 2

        def ahead(t):
            return t if isinstance(t, int) else t % NT

        def walk(eng, step):
            for half, c in PROLOGUE:
                if half == 0:
                    step(-2, c, 0)
                elif half == 1:
                    step(-1, c, 1, early_on=False)
                else:
                    step(-1, c, 1, main_on=False)
            for c in range(5):
                step(0, c, 0)
            with eng.Fori(0, NT // 2 - 1) as pair:
                T = pair * 2
                for c in range(5, CH):
                    step(T, c, 0)
                for c in range(CH):
                    step(T + 1, c, 1)
                for c in range(5):
                    step(T + 2, c, 0)
            for c in range(5, CH):
                step(NT - 2, c, 0)
            for c in range(CH):
                step(NT - 1, c, 1)
            for c in range(5):
                step(NT, c, 0)

        PROLOGUE = ((0, 8), (0, 9), (2, 3), (0, 10), (0, 11), (0, 12), (0, 13), (0, 14), (0, 15), (1, 0), (1, 1), (1, 2),
                    (1, 3), (1, 4), (2, 4), (1, 5), (1, 6), (2, 7), (2, 8), (1, 7), (2, 9), (1, 8), (2, 10), (1, 9),
                    (1, 10), (1, 11), (2, 11), (1, 12), (2, 12), (1, 13), (2, 13), (1, 14), (2, 14), (1, 15), (2, 15))

        def as_f32(ap):
            return ap.bitcast(F32)

        def folded(n):
            return (S_ps, O_ps, gate_ps[0], gate_ps[1])[n][0:CD, :].rearrange("p (q d) -> p q d", d=D)

        def a_bank(tile, q):
            return ((O_ps, S_ps, up_ps[0], up_ps[1]) if prologue(tile) else (O_ps, S_ps) * 2)[q]

        def xT_bank(tile):
            return up_ps[1] if prologue(tile) and not first(tile) else T_ps

        def s_bank(tile, k):
            return up_ps[0] if prologue(tile) and k % 2 else S_ps

        def b_bank(tile, q):
            return gate_ps[q] if prologue(tile) else O_ps

        def pT_bank(tile, k):
            return T_ps if k % 2 == 0 else y_ps if first(tile) else O_ps

        def ot_bank(tile, b):
            return up_ps[0] if first(tile) and b == 1 else O_ps

        block = stack.enter_context(nc.Block())

        @block.sync
        def _(sp):
            sp.dma_start(probs[:, 0, :, :].rearrange("p h j -> p (h j)"), Wq).then_inc(S["wq_loaded"], 16)
            sp.dma_start(probs[0:CD, 1, :, :].rearrange("p h j -> p (h j)"), Wk).then_inc(S["wk_loaded"], 16)
            sp.dma_start(x1[:, :, :, :].rearrange("p a k d -> p (a k d)")[:, 0:8 * CD].rearrange("p (s c) -> p s c", c=CD),
                         ctx_in.rearrange("b j c -> (b j) c").rearrange("(s p) c -> p s c", p=P)
                         ).then_inc(S["ctx_loaded"], 16)
            sp.dma_start(x_raw[:, 0, :, :], x_t[0]).then_inc(S["x_loaded"], 16)
            sp.dma_start(probs[0:CD, 2, :, :].rearrange("p h j -> p (h j)"), Wv).then_inc(S["wv_loaded"], 16)
            sp.dma_start(probs[:, 3, :, :].rearrange("p h j -> p (h j)").rearrange("p (s d) -> p s d", d=D),
                         Wout.rearrange("(s p) d -> p s d", p=P)).then_inc(S["wout_loaded"], 16)
            sp.dma_start(bgu_raw[0:CH, :], bg.rearrange("e (m p) -> (e m) p", p=P)).then_inc(S["small_loaded"], 16)
            sp.dma_start(bgu_raw[CH:2 * CH, :], bu.rearrange("e (m p) -> (e m) p", p=P)).then_inc(S["small_loaded"], 16)
            sp.dma_start(bout_col[:, :], bout.rearrange("(d a) -> d a", a=1)).then_inc(S["small_loaded"], 16)
            sp.dma_start(wr_raw[:, :], Wr).then_inc(S["small_loaded"], 16)
            for n in range(3):
                sp.dma_start(bo_raw[n * E:(n + 1) * E, :], bo).then_inc(S["bo_loaded"], 16)
            sp.wait_ge(S["x_loaded"], 16)
            sp.dma_start(x_raw[:, 1, :, :], x_t[1]).then_inc(S["x_loaded"], 16)
            sp.dma_start(wb[:, 0:4, :].rearrange("p a n -> p (a n)").rearrange("p (e m) -> p e m", e=E),
                         Wg.rearrange("e p m -> p e m")).then_inc(S["ffn_w_loaded"], 16)
            sp.dma_start(wb[:, 4:8, :].rearrange("p a n -> p (a n)").rearrange("p (e m) -> p e m", e=E),
                         Wu.rearrange("e p m -> p e m")).then_inc(S["ffn_w_loaded"], 16)
            sp.dma_start(ffn_tmp[:, 0:4, :].rearrange("p a n -> p (a n)").rearrange("p (c d) -> p c d", d=D),
                         Wo.rearrange("e (m p) d -> p (e m) d", p=P)).then_inc(S["ffn_w_loaded"], 16)
            sp.wait_ge(S["bo_lo_ready"], 1)
            sp.dma_start(as_f32(bo_hhl[0:2 * E, :]), as_f32(bo_hi[0:2 * E, :])).then_inc(S["bo_ready"], 16)
            sp.dma_start(as_f32(bo_hhl[2 * E:3 * E, :]), as_f32(bo_lo[2 * E:3 * E, :])).then_inc(S["bo_ready"], 16)
            sp.wait_ge(S["prep_ctx_lo"], 2)
            sp.dma_start(ctxT_dram[0][:, 0:NB * J], as_f32(ctxT_hi)).then_inc(S["ctxT_saved"], 16)
            sp.dma_start(ctxT_dram[1][:, 0:NB * J], as_f32(ctxT_lo)).then_inc(S["ctxT_saved"], 16)

            def step(T, c, odd, main_on=True, early_on=True):
                y_of, main, early = T - 1, T + 1 if main_on else None, T + 2 if early_on else None

                def index(t):
                    return t if isinstance(t, int) else sp.snap(t)

                if c == 4 and live(y_of):
                    at = index(y_of)
                    sp.wait_ge(S["y_added"], y_of + 1)
                    sp.dma_start(out_t[at], y_out[:, :, :]).then_inc(S["y_stored"], 16)
                if c == 7 and live(main) and live(T + 3):
                    at = index(ahead(T + 3))
                    sp.wait_ge(S["x1_ready"], main * 2 + 2)
                    sp.dma_start(x_raw[:, 1 - odd, :, :], x_t[at]).then_inc(S["x_loaded"], 16)
                if c in (8, 10) and live(early):
                    q = (c - 8) // 2
                    sp.wait_ge(S["b_lo_done"], early * 2 + q + 1)
                    wait(sp, "ot_ready", early * 2)
                    for b in range(BT):
                        for par in range(2):
                            for src, dst in ((bs_hi, b_hi), (bs_lo, b_lo)):
                                sp.dma_start(
                                    as_f32(dst[par * J:(par + 1) * J, b, 2 * q:2 * q + 2, :]),
                                    as_f32(src[b * J:(b + 1) * J, 4 * q:4 * q + 4, :]).rearrange(
                                        "p (n r) d -> p n r d", r=2)[:, :, par, :]).then_inc(S["b_moved"], 16)
                if c == 11 and live(early) and live(T + 3) and odd:
                    at = index(ahead(T + 3) * (BT * J))
                    if first(main):
                        sp.wait_ge(S["ctxT_saved"], 32)
                    sp.wait_ge(S["b_ready"], early * 2 + 2)
                    cols = slice(at, at + PAIR) if isinstance(T, int) else bass.ds(at, PAIR)
                    sp.dma_start(as_f32(ctxc_hi[:, :]), ctxT_dram[0][:, cols]).then_inc(S["ctxc_loaded"], 16)
                    sp.dma_start(as_f32(ctxc_lo[:, :]), ctxT_dram[1][:, cols]).then_inc(S["ctxc_loaded"], 16)
                if c == 14 and live(main):
                    sp.wait_ge(S["wT_done"], main * 2 + 1)
                    sp.dma_start(w_dram, wT[3 * E:4 * E, :]).then_inc(S["w_saved"], 16)
                    sp.wait_ge(S["w_saved"], main * 16 + 16)
                    if isinstance(main, int) and main == 0:
                        sp.wait_ge(S["w_lo_ready"], 2)
                    for n, (e0, e1) in enumerate(WB_PARTS):
                        if e1 == E:
                            wait(sp, "gw_done", T * CH + CH)
                        sp.dma_start(wb[:, e0:e1, :], w_dram[e0:e1, :].partition_broadcast(P)
                                     ).then_inc(S[f"wb_loaded{n}"], 16)

            walk(sp, step)
            sp.wait_ge(S["y_stored"], NT * 16)
            sp.wait_ge(S["x_loaded"], (NT + 1) * 16)
            sp.wait_ge(S["ctxc_loaded"], NT // 2 * 32)

        @block.tensor
        def _(pe):
            def mm3(o, w_h, w_l, m_h, m_l, start=True, stop=True):
                nc.tensor.matmul(o, w_h, m_h, start=start, stop=False)
                nc.tensor.matmul(o, w_h, m_l, start=False, stop=False)
                return nc.tensor.matmul(o, w_l, m_h, start=False, stop=stop)

            pe.wait_ge(S["ident_ready"], 2)
            pe.wait_ge(S["wq_loaded"], 16)
            for q in range(HP):
                last = nc.tensor.transpose(gate_ps[0][:, q * P:(q + 1) * P],
                                           probs[:, 0, 2 * q:2 * q + 2, :].rearrange("p h j -> p (h j)"), ident[:, :])
            last.then_inc(S["prep_T"], 1)
            pe.wait_ge(S["wk_loaded"], 16)
            for q in range(HP):
                last = nc.tensor.transpose(gate_ps[1][:, q * CD:(q + 1) * CD],
                                           probs[0:CD, 1, 2 * q:2 * q + 2, :].rearrange("p h j -> p (h j)"),
                                           ident[0:CD, 0:CD])
            last.then_inc(S["prep_T"], 1)
            pe.wait_ge(S["wqT_read"], 1)
            pe.wait_ge(S["wkT_read"], 1)
            wqT = y_out[:, :, :].rearrange("p k d -> p (k d)")
            for par in range(2):
                r = par * DH
                for q in range(HP):
                    last = nc.tensor.matmul((S_ps, O_ps)[par][0:CD, q * D:(q + 1) * D],
                                            ot_sb[r:r + DH, q * CD:(q + 1) * CD], wqT[r:r + DH, q * P:(q + 1) * P],
                                            start=True, stop=True)
                last.then_inc(S["prep_fold"], 1)
            pe.wait_ge(S["ctx_loaded"], 16)
            ctx_raw = x1[:, :, :, :].rearrange("p a k d -> p (a k d)")[:, 0:8 * CD].rearrange("p (s c) -> p s c", c=CD)
            for n in range(2):
                for s in range(4):
                    last = nc.tensor.transpose((up_ps[1], y_ps)[n][0:CD, s * P:(s + 1) * P], ctx_raw[:, 4 * n + s, :],
                                               ident[:, :])
                last.then_inc(S["prep_ctx_T"], 1)
            pe.wait_ge(S["wv_loaded"], 16)
            for q in range(HP):
                last = nc.tensor.transpose(up_ps[0][:, q * CD:(q + 1) * CD],
                                           probs[0:CD, 2, 2 * q:2 * q + 2, :].rearrange("p h j -> p (h j)"),
                                           ident[0:CD, 0:CD])
            last.then_inc(S["prep_T"], 1)

            def a_piece(early, q, ps):
                for i in range(2):
                    h = 2 * q + i
                    last = mm3(ps[:, i * PAIR:(i + 1) * PAIR], m_hi[:, h, :], m_lo[:, h, :], ctxc_hi[:, :], ctxc_lo[:, :])
                last.then_inc(S["a_ready"], 1)

            def xn_T(early):
                pe.wait_ge(S["xn_ready"], early + 1)
                for k in range(KT):
                    last = nc.tensor.transpose(xT_bank(early)[:, k * P:(k + 1) * P], xn[:, k, :], ident[:, :])
                last.then_inc(S["xT_ready"], 1)

            pe.wait_ge(S["prep_fold_lo"], 2)
            pe.wait_ge(S["ctxc_lo_done"], 1)
            for q in range(4):
                if q == 2:
                    pe.wait_ge(S["wvT_read"], 1)
                if q == 3:
                    pe.wait_ge(S["prep_ctx_lo"], 1)
                a_piece(0, q, a_bank(0, q))
            xn_T(0)
            pe.wait_ge(S["wvT_read"], 1)
            pe.wait_ge(S["wout_loaded"], 16)
            for par in range(2):
                r = par * DH
                for q in range(HP):
                    last = nc.tensor.matmul(gate_ps[par][0:CD, q * D:(q + 1) * D],
                                            yT_sb[r:r + DH, q * CD:(q + 1) * CD],
                                            probs[r:r + DH, 3, 2 * q:2 * q + 2, :].rearrange("p h j -> p (h j)"),
                                            start=True, stop=True)
                last.then_inc(S["prep_fold"], 1)
            pe.wait_ge(S["small_loaded"], 64)
            pe.wait_ge(S["xT_lo"], 1)
            nc.tensor.transpose(T_ps[:, 0:2 * CH], bgu_raw[:, :], ident[0:2 * CH, 0:2 * CH]).then_inc(S["bgu_T"], 1)

            def b_piece(early, odd_tile, q):
                w = slice(odd_tile * P, odd_tile * P + P)
                mm3(b_bank(early, q)[:, :], ctxc_hi[:, w], ctxc_lo[:, w],
                    n_hi[:, 4 * q:4 * q + 4, :].rearrange("p h d -> p (h d)"),
                    n_lo[:, 4 * q:4 * q + 4, :].rearrange("p h d -> p (h d)")).then_inc(S["b_ready"], 1)

            def scores(early, odd_tile, k):
                b = odd_tile * BT + k // 2
                w = slice(k * P, k * P + P)
                mm3(s_bank(early, k)[:, :], xnT_hi[:, w], xnT_lo[:, w], a_hi[:, b, :, :].rearrange("p h j -> p (h j)"),
                    a_lo[:, b, :, :].rearrange("p h j -> p (h j)")).then_inc(S["s_ready"], 1)

            def probs_T(a, k):
                pe.wait_ge(S["norm_done"], a * KT + k + 1)
                for q in range(HP):
                    last = nc.tensor.transpose(pT_bank(a, k)[:, q * P:(q + 1) * P],
                                               probs[:, k, 2 * q:2 * q + 2, :].rearrange("p h j -> p (h j)"),
                                               ident[:, :])
                last.then_inc(S["pT_ready"], 1)

            def attn_out(a, b):
                w = slice(b * SEQ, (b + 1) * SEQ)
                for q in range(HP):
                    last = mm3(ot_bank(a, b)[:, w], b_hi[:, b, q, :], b_lo[:, b, q, :], pT_hi[:, q, w], pT_lo[:, q, w],
                               start=(q == 0), stop=(q == HP - 1))
                last.then_inc(S["ot_ready"], 1)

            def step(T, c, odd, main_on=True, early_on=True):
                y_of, main, early = T - 1, T + 1 if main_on else None, T + 2 if early_on else None
                if live(T):
                    n = T * CH + c
                    rhs_h, rhs_l = xn2T_hi[:, odd, :], xn2T_lo[:, odd, :]
                    if c == 0:
                        pe.wait_ge(S["x2T_lo"], T + 1)
                    if c == 0 and isinstance(T, int) and T == 0:
                        pe.wait_ge(S["w_lo_ready"], 3)
                        pe.wait_ge(S["w_hi_ready"], 3)
                    wait(pe, "gate_done", n - 1)
                    mm3(gate_ps[c % 2][:, :], wg_hi[:, c, :], wg_lo[:, c, :], rhs_h, rhs_l).then_inc(S["gate_ready"], 1)
                    wait(pe, "h_done", n - 1)
                    mm3(up_ps[c % 2][:, :], wu_hi[:, c, :], wu_lo[:, c, :], rhs_h, rhs_l).then_inc(S["up_ready"], 1)
                t, d = (T, c - LAG) if c >= LAG else (T - 1, c - LAG + CH)
                if live(t):
                    if d == 0:
                        wait(pe, "y_read", t)
                        pe.wait_ge(S["wT_done"], t * 2 + 2)
                        if isinstance(t, int) and t == 0:
                            pe.wait_ge(S["bo_ready"], 32)
                            pe.wait_ge(S["prep_ctx_lo"], 2)
                        nc.tensor.matmul(y_ps[:, :], bo_hhl[:, :], wT_r[0:3 * E, :], start=True, stop=False)
                    pe.wait_ge(S["h_lo_done"], t * CH + d + 1)
                    mm3(y_ps[:, :], wo_hi[:, d, :], wo_lo[:, d, :], h_hi[:, d % NHB, :], h_lo[:, d % NHB, :],
                        start=False, stop=(d == CH - 1)).then_inc(S["down_done"], 1)

                if live(early):
                    if c in (5, 6) and not odd:
                        if c == 5:
                            pe.wait_ge(S["ctxc_loaded"], early * 16)
                            pe.wait_ge(S["ot_read"], early * 2)
                            pe.wait_ge(S["s_sub"], early * KT)
                        else:
                            pe.wait_ge(S["a_lo_done"], early * 2 + 2)
                        for q in (2 * (c - 5), 2 * (c - 5) + 1):
                            a_piece(early, q, a_bank(early, q))
                    if c == 7:
                        if not prologue(early):
                            pe.wait_ge(S["x1_ready"], early * 2)
                        xn_T(early)
                    if 8 <= c < 8 + KT:
                        k = c - 8
                        if k == 0:
                            pe.wait_ge(S["xT_lo"], early + 1)
                            pe.wait_ge(S["a_lo_done"], early * 2 + 4 if not odd else early * 2 + 2)
                        elif not prologue(early):
                            pe.wait_ge(S["s_sub"], early * KT + k)
                        elif k > 1:
                            pe.wait_ge(S["s_sub"], early * KT + k - 1)
                        scores(early, odd, k)
                    if c in (8, 10):
                        q = (c - 8) // 2
                        if prologue(early):
                            pe.wait_ge(S["prep_fold_lo"], 4)
                            wait(pe, "b_lo_done", early * 2)
                        elif q == 0:
                            wait(pe, "ot_read", early * 2)
                        else:
                            pe.wait_ge(S["b_lo_done"], early * 2 + 1)
                        b_piece(early, odd, q)
                if live(main):
                    if c == 0:
                        wait(pe, "wT_done", main * 2)
                        probs_T(main, 1)
                        pe.wait_ge(S["pT_lo_done"], main * KT + 1)
                        probs_T(main, 2)
                    if c == 1:
                        pe.wait_ge(S["pT_lo_done"], main * KT + 2)
                        probs_T(main, 3)
                if live(main):
                    if c == 2:
                        pe.wait_ge(S["b_moved"], main * 256 + 256)
                        pe.wait_ge(S["pT_lo_done"], main * KT + (2 if first(main) else 4))
                        attn_out(main, 0)
                    if c == 4:
                        pe.wait_ge(S["pT_lo_done"], main * KT + 4)
                        if not first(main):
                            pe.wait_ge(S["ot_read"], main * 2 + 1)
                        attn_out(main, 1)
                if c == 3 and live(y_of):
                    pe.wait_ge(S["y_read"], y_of + 1)
                    if live(main):
                        pe.wait_ge(S["pT_lo_done"], main * KT + 4)
                    for k in range(KT):
                        last = nc.tensor.transpose(T_ps[:, k * P:(k + 1) * P], yT_sb[:, k * P:(k + 1) * P], ident[:, :])
                    last.then_inc(S["yT_ready"], 1)
                if live(main):
                    if c in (4, 5):
                        b = c - 4
                        pe.wait_ge(S["ot_read"], main * 2 + b + 1)
                        if b == 0 and live(y_of):
                            pe.wait_ge(S["y_added"], y_of + 1)
                        if b == 1:
                            pe.wait_ge(S["x1_ready"], main * 2 + 1)
                        for k in (2 * b, 2 * b + 1):
                            last = nc.tensor.transpose(T_ps[:, k * P:(k + 1) * P], ot_sb[:, k * P:(k + 1) * P],
                                                       ident[:, :])
                        last.then_inc(S["ott_ready"], 1)
                    if c == 8:
                        if live(early):
                            pe.wait_ge(S["xT_lo"], early + 1)
                        pe.wait_ge(S["xn2_ready"], main + 1)
                        for k in range(KT):
                            last = nc.tensor.transpose(T_ps[:, k * P:(k + 1) * P], xn2[:, k, :], ident[:, :])
                        last.then_inc(S["x2T_ready"], 1)
                    if c == 11:
                        pe.wait_ge(S["x2T_lo"], main + 1)
                        if live(early):
                            pe.wait_ge(S["b_lo_done"], early * 2 + 2)
                        if isinstance(main, int) and main == 0:
                            pe.wait_ge(S["wr_ready"], 1)
                        for k in range(KT):
                            w = slice(k * P, k * P + P)
                            o = O_ps[:, 2 * E * k:2 * E * (k + 1)]
                            nc.tensor.matmul(o, xn2T_hi[:, 1 - odd, w], wr_hl[:, :, :].rearrange("p a e -> p (a e)"),
                                             start=True, stop=False)
                            last = nc.tensor.matmul(o[:, 0:E], xn2T_lo[:, 1 - odd, w], wr_hl[:, 0, :],
                                                    start=False, stop=True)
                        last.then_inc(S["router_ready"], 1)
                    if c == 14:
                        pe.wait_ge(S["w_ready"], main + 1)
                        for k in range(KT):
                            last = nc.tensor.transpose(O_ps[0:4 * E, k * P:(k + 1) * P], wst[:, k, :], ident[:, :])
                        last.then_inc(S["wT_ready"], 1)
                if c == 15 and live(early):
                    if first(early):
                        pe.wait_ge(S["bgu_ready"], 1)
                        pe.wait_ge(S["prep_ctx_lo"], 2)
                    probs_T(early, 0)

            walk(pe, step)

        @block.scalar
        def _(act):
            copy = nc.scalar.copy
            act.wait_ge(S["prep_T"], 1)
            copy(y_out[:, :, :].rearrange("p k d -> p (k d)"), gate_ps[0][:, :]).then_inc(S["wqT_read"], 1)

            def fold_hi(n):
                act.wait_ge(S["prep_fold"], n + 1)
                dst = (m_hi, m_hi, n_hi, n_hi)[n][:, :, :].rearrange("p (q r) d -> p r q d", r=2)[:, n % 2, :, :]
                nc.scalar.mul(dst, folded(n), SCALE if n < 2 else 1.0).then_inc(S["prep_fold_hi"], 1)

            def xn_apply(early, odd):
                act.wait_ge(S["ln1_rstd"], early + 1)
                act.wait_ge(S["x_loaded"], early * 16 + 16)
                for k in range(KT):
                    last = nc.scalar.activation(xn[:, k, :], x_raw[:, odd, k, :], ACT.Identity,
                                                bias=nmr[:, k:k + 1], scale=rstd[:, k:k + 1])
                last.then_inc(S["xn_ready"], 1)

            def a_hi_part(early, q):
                act.wait_ge(S["a_ready"], early * 2 + q + 1)
                copy(a_hi[:, :, 2 * q:2 * q + 2, :].rearrange("p b h j -> p h b j"),
                     a_bank(early, q)[:, :].rearrange("p (h b j) -> p h b j", h=2, j=J)).then_inc(S["a_hi_done"], 1)

            def xT_hi_part(early):
                act.wait_ge(S["xT_ready"], early + 1)
                copy(xnT_hi[:, :], xT_bank(early)[:, :]).then_inc(S["xT_hi"], 1)

            fold_hi(0)
            fold_hi(1)
            act.wait_ge(S["prep_ctx_T"], 1)
            copy(ctxc_hi[:, :], up_ps[1][0:CD, 0:PAIR])
            copy(ctxT_hi[:, 0:512], up_ps[1][0:CD, :]).then_inc(S["prep_ctx_hi"], 1)
            xn_apply(0, 0)
            act.wait_ge(S["prep_T"], 3)
            copy(yT_sb[:, 0:HP * CD], up_ps[0][:, 0:HP * CD]).then_inc(S["wvT_read"], 1)
            for q in range(4):
                a_hi_part(0, q)
            xT_hi_part(0)
            act.wait_ge(S["prep_ctx_T"], 2)
            copy(ctxT_hi[:, 512:1024], y_ps[0:CD, :]).then_inc(S["prep_ctx_hi"], 1)
            fold_hi(2)
            fold_hi(3)
            act.wait_ge(S["bgu_T"], 1)
            copy(bgu[:, :, :].rearrange("p a c -> p (a c)"), T_ps[:, 0:2 * CH]).then_inc(S["bgu_ready"], 1)
            act.wait_ge(S["small_loaded"], 64)
            copy(wr_hl[:, 0, :], wr_raw[:, :]).then_inc(S["wr_hi_ready"], 1)
            act.wait_ge(S["bo_loaded"], 48)
            copy(bo_hi[:, :], bo_raw[:, :]).then_inc(S["bo_hi_ready"], 1)

            def hidden_hi(T, c):
                t, d = (T, c - 1) if c >= 1 else (T - 1, CH - 1)
                if live(t):
                    act.wait_ge(S["h_done"], t * CH + d + 1)
                    wait(act, "down_done", t * CH + d - NHB + 1)
                    copy(h_hi[:, d % NHB, :], h_sb(d)).then_inc(S["h_hi_done"], 1)

            def step(T, c, odd, main_on=True, early_on=True):
                y_of, main, early = T - 1, T + 1 if main_on else None, T + 2 if early_on else None
                if c == 3 and live(y_of):
                    act.wait_ge(S["down_done"], y_of * CH + CH)
                    copy(yT_sb[:, :], y_ps[:, :]).then_inc(S["y_read"], 1)
                if live(T):
                    n = T * CH + c
                    act.wait_ge(S["gate_ready"], n + 1)
                    wait(act, "gw_done", n - 1)
                    nc.scalar.activation(gate_sb(c), gate_ps[c % 2][:, :], ACT.Silu, bias=bgu[:, 0, c:c + 1]
                                         ).then_inc(S["gate_done"], 1)
                if c == 12:
                    for i in range(2):
                        if live(early):
                            act.wait_ge(S["s_sub"], early * KT + 2 * i + 2)
                            nc.scalar.activation(probs[:, 2 * i:2 * i + 2, :, :], probs[:, 2 * i:2 * i + 2, :, :],
                                                 ACT.Exp).then_inc(S["exp_done"], 1)
                        if live(main) and i == 0:
                            act.wait_ge(S["logits_ready"], main + 1)
                            nc.scalar.activation(lg_e[:, :, :], lg_d[:, :, :], ACT.Exp).then_inc(S["route_exp"], 1)
                        if i == 0:
                            hidden_hi(T, c)
                elif c not in (1, 14):
                    hidden_hi(T, c)
                if live(main) and c == 14:
                    act.wait_ge(S["wT_ready"], main + 1)
                    wait(act, "w_saved", main * 16)
                    copy(wT[:, :], O_ps[0:4 * E, :]).then_inc(S["wT_done"], 1)
                    copy(wT_r[:, :], O_ps[0:4 * E, :]).then_inc(S["wT_done"], 1)
                if c == 14:
                    hidden_hi(T, c)
                if first(early) and c in (9, 10, 12):
                    if c == 9:
                        act.wait_ge(S["ffn_w_loaded"], 48)
                    w, src = ((wg_hi, wb[:, 0:4, :]), (wu_hi, wb[:, 4:8, :]), (wo_hi, ffn_tmp[:, 0:4, :]))[min(c - 9, 2)]
                    copy(w[:, :, :].rearrange("p c n -> p (c n)"), src.rearrange("p a n -> p (a n)")
                         ).then_inc(S["w_hi_ready"], 1)
                if live(early):
                    if c == 4:
                        xn_apply(early, odd)
                    if c in (5, 6) and not odd:
                        a_hi_part(early, 2 * (c - 5))
                        a_hi_part(early, 2 * (c - 5) + 1)
                    if c == 7:
                        xT_hi_part(early)
                if live(main) and c == 7:
                    act.wait_ge(S["ln2_rstd"], main + 1)
                    for k in range(KT):
                        last = nc.scalar.activation(xn2[:, k, :], x1[:, 1 - odd, k, :], ACT.Identity,
                                                    bias=nmr[:, KT + k:KT + k + 1], scale=rstd[:, KT + k:KT + k + 1])
                    last.then_inc(S["xn2_ready"], 1)
                if live(early):
                    if c in (8, 10):
                        q = (c - 8) // 2
                        act.wait_ge(S["b_ready"], early * 2 + q + 1)
                        wait(act, "b_moved", early * 256)
                        copy(bs_hi[:, 4 * q:4 * q + 4, :].rearrange("p h d -> p (h d)"), b_bank(early, q)[:, :]
                             ).then_inc(S["b_hi_done"], 1)
                for a, k, on in ((early, 0, c == 15), (main, 1, c == 0), (main, 2, c == 0), (main, 3, c == 1)):
                    if on and live(a):
                        act.wait_ge(S["pT_ready"], a * KT + k + 1)
                        if first(a) and k == 0:
                            act.wait_ge(S["ctxT_saved"], 32)
                        copy(pT_hi[:, :, k * P:(k + 1) * P], pT_bank(a, k)[:, :].rearrange("p (q n) -> p q n", q=HP)
                             ).then_inc(S["pT_hi_done"], 1)
                if c == 1:
                    hidden_hi(T, c)
                if live(main):
                    if c in (2, 4):
                        b = (c - 2) // 2
                        act.wait_ge(S["ot_ready"], main * 2 + b + 1)
                        w = slice(b * SEQ, (b + 1) * SEQ)
                        nc.scalar.activation(ot_sb[:, w], ot_bank(main, b)[:, w], ACT.Identity, bias=bout_col[:, 0:1]
                                             ).then_inc(S["ot_read"], 1)
                    if c == 8:
                        act.wait_ge(S["x2T_ready"], main + 1)
                        copy(xn2T_hi[:, 1 - odd, :], T_ps[:, :]).then_inc(S["x2T_hi"], 1)

            walk(act, step)

        @block.gpsimd
        def _(pool):
            nc.gpsimd.memset(ident[:, :], 0.0).then_inc(S["ident_ready"], 1)
            pool.wait_ge(S["ident_ready"], 1)
            nc.gpsimd.affine_select(out=ident[:, :], in_=ident[:, :], compare_op=ALU.not_equal, fill=1.0, base=0,
                                    pattern=[[-1, P]], channel_multiplier=1).then_inc(S["ident_ready"], 1)
            nc.gpsimd.memset(m_half[:, :], -0.5).then_inc(S["half_ready"], 1)
            nc.gpsimd.iota(iota_e[:, :, :], [[0, KT], [1, E]], base=0, channel_multiplier=0,
                           allow_small_or_imprecise_dtypes=True).then_inc(S["iota_ready"], 1)
            pool.wait_ge(S["small_loaded"], 64)
            pool.wait_ge(S["half_ready"], 1)

            def w_lo(n):
                hi, lo, src = ((wg_hi, wg_lo, wb[:, 0:4, :]), (wu_hi, wu_lo, wb[:, 4:8, :]),
                               (wo_hi, wo_lo, ffn_tmp[:, 0:4, :]))[n]
                pool.wait_ge(S["w_hi_ready"], n + 1)
                nc.gpsimd.tensor_tensor(lo[:, :, :].rearrange("p c n -> p (c n)"), src.rearrange("p a n -> p (a n)"),
                                        as_f32(hi[:, :, :].rearrange("p c n -> p (c n)")), ALU.subtract
                                        ).then_inc(S["w_lo_ready"], 1)

            def ln1_rstd(early):
                pool.wait_ge(S["ln1_stats"], early * 4 + 4)
                nc.gpsimd.tensor_tensor(rstd[:, 0:KT], var_eps[:, 0:KT], m_half[:, 0:KT], ALU.pow
                                        ).then_inc(S["ln1_pow"], 1)
                pool.wait_ge(S["ln1_pow"], early + 1)
                nc.gpsimd.tensor_tensor(nmr[:, 0:KT], neg_mean[:, 0:KT], rstd[:, 0:KT], ALU.mult
                                        ).then_inc(S["ln1_rstd"], 1)

            ln1_rstd(0)

            def step(T, c, odd, main_on=True, early_on=True):
                main, early = T + 1 if main_on else None, T + 2 if early_on else None
                if live(early) and c == 4:
                    ln1_rstd(early)
                if live(main) and c == 0:
                    norm(main, 3)
                if live(T):
                    n = T * CH + c
                    for part, (e0, _) in enumerate(WB_PARTS):
                        if c == e0 * MC:
                            pool.wait_ge(S[f"wb_loaded{part}"], T * 16 + 16)
                    pool.wait_ge(S["gate_done"], n + 1)
                    wait(pool, "h_done", n - 1)
                    nc.gpsimd.tensor_tensor(gw_sb(c), gate_sb(c), wb[:, c // MC, :], ALU.mult).then_inc(S["gw_done"], 1)
                if live(early):
                    if first(early) and c == 9:
                        w_lo(0)
                    if c == 13:
                        norm(early, 0)
                    if c == 14:
                        norm(early, 1)
                    if c == 15:
                        norm(early, 2)
                if live(main):
                    if first(main) and c in (1, 7):
                        w_lo(1 if c == 1 else 2)
                    if c == 6:
                        w = slice(KT, 2 * KT)
                        pool.wait_ge(S["ln2_stats"], main * 4 + 4)
                        nc.gpsimd.tensor_tensor(rstd[:, w], var_eps[:, w], m_half[:, w], ALU.pow
                                                ).then_inc(S["ln2_pow"], 1)
                        pool.wait_ge(S["ln2_pow"], main + 1)
                        nc.gpsimd.tensor_tensor(nmr[:, w], neg_mean[:, w], rstd[:, w], ALU.mult
                                                ).then_inc(S["ln2_rstd"], 1)

            def norm(a, k):
                pool.wait_ge(S["inv_done"], a * 2 + k // 2 + 1)
                nc.gpsimd.tensor_tensor(probs[:, k, :, :], probs[:, k, :, :],
                                        r_inv[:, k, :].unsqueeze(2).to_broadcast([P, H, J]), ALU.mult
                                        ).then_inc(S["norm_done"], 1)

            walk(pool, step)

        @block.vector
        def _(dve):
            V = nc.vector

            def stats(src, col, ks, base, name):
                for k in ks:
                    last = V.bn_stats(bn[:, col + k, :], src(k))
                last.then_inc(S[name], 1)
                w = slice(col + ks[0], col + ks[-1] + 1)
                dve.wait_ge(S[name], base + 1)
                V.tensor_tensor(m_diff[:, w], bn[:, w, 1], bn[:, w, 4], ALU.subtract)
                V.tensor_tensor(v_sum[:, w], bn[:, w, 2], bn[:, w, 5], ALU.add).then_inc(S[name], 1)
                dve.wait_ge(S[name], base + 2)
                V.scalar_tensor_tensor(m_sq[:, w], m_diff[:, w], 0.25, m_diff[:, w], ALU.mult, ALU.mult)
                V.tensor_scalar(v_eps[:, w], v_sum[:, w], 1.0 / D, EPS, ALU.mult, ALU.add)
                V.scalar_tensor_tensor(neg_mean[:, w], m_diff[:, w], -0.5, bn[:, w, 4], ALU.mult, ALU.subtract
                                       ).then_inc(S[name], 1)
                dve.wait_ge(S[name], base + 3)
                V.tensor_tensor(var_eps[:, w], v_eps[:, w], m_sq[:, w], ALU.add).then_inc(S[name], 1)

            def split_lo(lo, full, hi):
                return V.tensor_tensor(lo, full, as_f32(hi), ALU.subtract)

            def a_lo_part(early, q):
                dve.wait_ge(S["a_hi_done"], early * 2 + q + 1)
                w = (slice(None), slice(None), slice(2 * q, 2 * q + 2), slice(None))
                split_lo(a_lo[w].rearrange("p b h j -> p h b j"),
                         a_bank(early, q)[:, :].rearrange("p (h b j) -> p h b j", h=2, j=J),
                         a_hi[w].rearrange("p b h j -> p h b j")).then_inc(S["a_lo_done"], 1)

            def xT_lo_part(early):
                dve.wait_ge(S["xT_hi"], early + 1)
                split_lo(xnT_lo[:, :], xT_bank(early)[:, :], xnT_hi[:, :]).then_inc(S["xT_lo"], 1)

            def ctx_lo(n):
                dve.wait_ge(S["prep_ctx_hi"], n + 1)
                w = slice(n * 512, (n + 1) * 512)
                V.tensor_tensor(ctxT_lo[:, w], (up_ps[1], y_ps)[n][0:CD, :], as_f32(ctxT_hi[:, w]), ALU.subtract
                                ).then_inc(S["prep_ctx_lo"], 1)

            def fold_lo(n):
                dve.wait_ge(S["prep_fold_hi"], n + 1)
                hi, lo = ((m_hi, m_lo), (m_hi, m_lo), (n_hi, n_lo), (n_hi, n_lo))[n]
                hi, lo = (w[:, :, :].rearrange("p (q r) d -> p r q d", r=2)[:, n % 2, :, :] for w in (hi, lo))
                V.scalar_tensor_tensor(lo, folded(n), SCALE if n < 2 else 1.0, as_f32(hi), ALU.mult, ALU.subtract
                                       ).then_inc(S["prep_fold_lo"], 1)

            def ln1_stats(early, odd):
                dve.wait_ge(S["x_loaded"], early * 16 + 16)
                wait(dve, "ln1_rstd", early)
                stats(lambda k: x_raw[:, odd, k, :], 0, range(KT), early * 4, "ln1_stats")

            dve.wait_ge(S["prep_T"], 2)
            V.tensor_copy(ot_sb[:, 0:HP * CD], gate_ps[1][:, 0:HP * CD]).then_inc(S["wkT_read"], 1)
            ln1_stats(0, 0)
            fold_lo(0)
            fold_lo(1)
            dve.wait_ge(S["prep_ctx_hi"], 1)
            V.tensor_tensor(ctxc_lo[:, :], up_ps[1][0:CD, 0:PAIR], as_f32(ctxc_hi[:, :]), ALU.subtract
                            ).then_inc(S["ctxc_lo_done"], 1)
            ctx_lo(0)
            for q in range(4):
                a_lo_part(0, q)
            xT_lo_part(0)
            ctx_lo(1)
            fold_lo(2)
            fold_lo(3)
            dve.wait_ge(S["wr_hi_ready"], 1)
            V.tensor_tensor(wr_hl[:, 1, :], wr_raw[:, :], as_f32(wr_hl[:, 0, :]), ALU.subtract).then_inc(S["wr_ready"], 1)
            dve.wait_ge(S["bo_hi_ready"], 1)
            V.tensor_tensor(bo_lo[:, :], bo_raw[:, :], as_f32(bo_hi[:, :]), ALU.subtract).then_inc(S["bo_lo_ready"], 1)
            dve.wait_ge(S["iota_ready"], 1)
            dve.wait_ge(S["bgu_ready"], 1)

            ROUTE = 8

            def step(T, c, odd, main_on=True, early_on=True):
                y_of, main, early = T - 1, T + 1 if main_on else None, T + 2 if early_on else None

                for a, k, on in ((main, 0, c == 0), (main, 1, c == 1), (main, 2, c == 1), (main, 3, c == 2)):
                    if on and live(a):
                        dve.wait_ge(S["pT_hi_done"], a * KT + k + 1)
                        split_lo(pT_lo[:, :, k * P:(k + 1) * P], pT_bank(a, k)[:, :].rearrange("p (q n) -> p q n", q=HP),
                                 pT_hi[:, :, k * P:(k + 1) * P]).then_inc(S["pT_lo_done"], 1)
                if c == 4 and live(y_of):
                    dve.wait_ge(S["yT_ready"], y_of + 1)
                    V.tensor_tensor(y_out[:, :, :].rearrange("p k d -> p (k d)"), T_ps[:, :],
                                    x1[:, 1 - odd, :, :].rearrange("p k d -> p (k d)"), ALU.add).then_inc(S["y_added"], 1)
                if live(main):
                    if c in (5, 6):
                        b = c - 5
                        dve.wait_ge(S["ott_ready"], main * 2 + b + 1)
                        dve.wait_ge(S["x_loaded"], main * 16 + 16)
                        V.tensor_tensor(x1[:, 1 - odd, 2 * b:2 * b + 2, :],
                                        T_ps[:, b * SEQ:(b + 1) * SEQ].rearrange("p (k d) -> p k d", d=D),
                                        x_raw[:, 1 - odd, 2 * b:2 * b + 2, :], ALU.add).then_inc(S["x1_ready"], 1)
                if live(early):
                    if c == 8 and not first(early):
                        xT_lo_part(early)
                    if c in (6, 7) and not odd:
                        a_lo_part(early, 2 * (c - 6))
                        a_lo_part(early, 2 * (c - 6) + 1)
                    if 9 <= c < 9 + KT:
                        k = c - 9
                        s3 = s_bank(early, k)[:, :].rearrange("p (h j) -> p h j", h=H)
                        dve.wait_ge(S["s_ready"], early * KT + k + 1)
                        V.tensor_reduce(s_max[:, k, :], s3, AX_X, ALU.max).then_inc(S["s_maxed"], 1)
                        dve.wait_ge(S["s_maxed"], early * KT + k + 1)
                        V.tensor_tensor(probs[:, k, :, :], s3, s_max[:, k, :].unsqueeze(2).to_broadcast([P, H, J]),
                                        ALU.subtract).then_inc(S["s_sub"], 1)
                if live(main) and c == 10:
                    dve.wait_ge(S["x2T_hi"], main + 1)
                    split_lo(xn2T_lo[:, 1 - odd, :], T_ps[:, :], xn2T_hi[:, 1 - odd, :]).then_inc(S["x2T_lo"], 1)
                if live(early) and c in (9, 11):
                    q = (c - 9) // 2
                    dve.wait_ge(S["b_hi_done"], early * 2 + q + 1)
                    w = slice(4 * q, 4 * q + 4)
                    split_lo(bs_lo[:, w, :].rearrange("p h d -> p (h d)"), b_bank(early, q)[:, :],
                             bs_hi[:, w, :].rearrange("p h d -> p (h d)")).then_inc(S["b_lo_done"], 1)
                if c == 12:
                    hidden(T, c)
                    hidden_lo(T, c)
                if live(main) and c == 12:
                    at = main * ROUTE
                    o = O_ps[:, 0:KT * 2 * E].rearrange("p (k a e) -> p k a e", k=KT, a=2)
                    dve.wait_ge(S["router_ready"], main + 1)
                    V.tensor_copy(lg_lo[:, :, :], o[:, :, 1, :]).then_inc(S["route_step"], 1)
                    dve.wait_ge(S["route_step"], at + 1)
                    V.tensor_tensor(lg[:, :, :], o[:, :, 0, :], lg_lo[:, :, :], ALU.add).then_inc(S["route_step"], 1)
                    dve.wait_ge(S["route_step"], at + 2)
                    V.tensor_copy(lg_lo[:, :, :], lg[:, :, :])
                    for k in range(KT):
                        last = V.max(top[:, k, :], lg[:, k, :])
                    last.then_inc(S["route_step"], 1)
                    dve.wait_ge(S["route_step"], at + 3)
                    V.tensor_tensor(lg_d[:, :, :], lg[:, :, :], top[:, :, 0:1].to_broadcast([P, KT, E]), ALU.subtract
                                    ).then_inc(S["logits_ready"], 1)
                if live(y_of) and c == 14:
                    dve.wait_ge(S["y_stored"], y_of * 16 + 16)
                if c != 12:
                    hidden(T, c)
                if c != 12:
                    hidden_lo(T, c)
                if live(early) and c == 3:
                    ln1_stats(early, odd)
                if live(main) and c == 6:
                    dve.wait_ge(S["x1_ready"], main * 2 + 2)
                    stats(lambda k: x1[:, 1 - odd, k, :], KT, range(KT), main * 4, "ln2_stats")
                if live(main) and c == 12:
                    at = main * ROUTE
                    for k in range(KT):
                        last = V.max_index(top_at[:, k, :], top[:, k, :], lg[:, k, :])
                    last.then_inc(S["route_step"], 1)
                    dve.wait_ge(S["route_step"], at + 4)
                    V.tensor_tensor(oh1[:, :, :], iota_e[:, :, :], top_at[:, :, 0:1].to_broadcast([P, KT, E]),
                                    ALU.is_equal)
                    V.tensor_tensor(oh2[:, :, :], iota_e[:, :, :], top_at[:, :, 1:2].to_broadcast([P, KT, E]),
                                    ALU.is_equal).then_inc(S["route_step"], 1)
                    dve.wait_ge(S["route_step"], at + 5)
                    V.tensor_tensor(sel[:, :, :], oh1[:, :, :], oh2[:, :, :], ALU.add).then_inc(S["route_step"], 1)
                if live(main) and c == 13:
                    at = main * ROUTE
                    dve.wait_ge(S["route_exp"], main + 1)
                    dve.wait_ge(S["route_step"], at + 6)
                    V.tensor_tensor(sel_e[:, :, :], sel[:, :, :], lg_e[:, :, :], ALU.mult)
                    V.tensor_reduce(den_a[:, :], lg_e[:, :, :], AX_X, ALU.add).then_inc(S["route_step"], 1)
                    dve.wait_ge(S["route_step"], at + 7)
                    V.tensor_reduce(den_b[:, :], sel_e[:, :, :], AX_X, ALU.add).then_inc(S["route_step"], 1)
                    dve.wait_ge(S["route_step"], at + 8)
                    V.scalar_tensor_tensor(den[:, :], den_a[:, :], NORM_EPS, den_b[:, :], ALU.mult, ALU.add
                                           ).then_inc(S["w_steps"], 1)
                    dve.wait_ge(S["w_steps"], main * 3 + 1)
                    V.reciprocal(den_inv[:, :], den[:, :]).then_inc(S["w_steps"], 1)
                    dve.wait_ge(S["w_steps"], main * 3 + 2)
                    V.tensor_tensor(wst[:, :, 3 * E:4 * E], sel_e[:, :, :],
                                    den_inv[:, :].unsqueeze(2).to_broadcast([P, KT, E]), ALU.mult)
                    V.tensor_tensor(wst[:, :, 0:E].bitcast(F32R), sel_e[:, :, :],
                                    den_inv[:, :].unsqueeze(2).to_broadcast([P, KT, E]), ALU.mult)
                    V.tensor_tensor(wst[:, :, 2 * E:3 * E].bitcast(F32R), sel_e[:, :, :],
                                    den_inv[:, :].unsqueeze(2).to_broadcast([P, KT, E]), ALU.mult
                                    ).then_inc(S["w_steps"], 1)
                    dve.wait_ge(S["w_steps"], main * 3 + 3)
                    V.tensor_tensor(wst[:, :, E:2 * E], wst[:, :, 3 * E:4 * E], wst[:, :, 0:E], ALU.subtract
                                    ).then_inc(S["w_ready"], 1)
                if live(early) and c in (13, 14):
                    sums(early, c - 13)

            def hidden(T, c):
                t, d = (T, c - 1) if c >= 1 else (T - 1, c - 1 + CH)
                if live(t):
                    dve.wait_ge(S["gw_done"], t * CH + d + 1)
                    dve.wait_ge(S["up_ready"], t * CH + d + 1)
                    wait(dve, "h_lo_done", t * CH + d - 1)
                    V.scalar_tensor_tensor(h_sb(d), up_ps[d % 2][:, :], bgu[:, 1, d:d + 1], gw_sb(d), ALU.add, ALU.mult
                                           ).then_inc(S["h_done"], 1)

            def hidden_lo(T, c):
                t, d = (T, c - 2) if c >= 2 else (T - 1, c - 2 + CH)
                if live(t):
                    dve.wait_ge(S["h_hi_done"], t * CH + d + 1)
                    split_lo(h_lo[:, d % NHB, :], h_sb(d), h_hi[:, d % NHB, :]).then_inc(S["h_lo_done"], 1)

            def sums(a, i):
                w = slice(2 * i, 2 * i + 2)
                dve.wait_ge(S["exp_done"], a * 2 + i + 1)
                V.tensor_reduce(r_sum[:, w, :], probs[:, w, :, :], AX_X, ALU.add).then_inc(S["sums_done"], 1)
                dve.wait_ge(S["sums_done"], a * 2 + i + 1)
                V.reciprocal(r_inv[:, w, :], r_sum[:, w, :]).then_inc(S["inv_done"], 1)

            walk(dve, step)


_INS = ['x', 'ctx_768', 'L0_xattn_Wq', 'L0_xattn_Wk', 'L0_xattn_Wv', 'L0_xattn_Wout', 'L0_xattn_bout',
        'L0_ffn_W_router', 'L0_ffn_W_gate', 'L0_ffn_b_gate', 'L0_ffn_W_up', 'L0_ffn_b_up', 'L0_ffn_W_out',
        'L0_ffn_b_out']
_OUTS = [((16, 256, 128), 'float32')]


def kernel(**inputs):
    import numpy as _np
    import concourse.bacc as _bacc
    from concourse import mybir as _mybir
    from concourse.bass_utils import run_bass_kernel_spmd as _run

    nc = _bacc.Bacc("TRN2", target_bir_lowering=False, num_devices=1)
    arrays, args = {}, []
    for name in _INS:
        a = _np.ascontiguousarray(inputs[name])
        arrays[f"in_{name}_dram"] = a
        args.append(nc.dram_tensor(f"in_{name}_dram", a.shape, _mybir.dt.from_np(a.dtype), kind="ExternalInput").ap())
    for i, (shape, dtype) in enumerate(_OUTS):
        dt = _mybir.dt.from_np(_np.dtype(dtype))
        args.append(nc.dram_tensor(f"out_{i}_dram", shape, dt, kind="ExternalOutput").ap())
    xattn_moe_kernel(nc, *args)
    r = _run(nc, [arrays], core_ids=[0])
    got = tuple(r.results[0][f"out_{i}_dram"] for i in range(len(_OUTS)))
    return got[0]
```
